# Optimizing a Trainium2 kernel written in Bass

```python
import numpy as np
import jax
import jax.numpy as jnp

def _softmax(x, axis=-1):
    return jax.nn.softmax(x, axis=axis)

def _gelu(x):
    return jax.nn.gelu(x, approximate=True)

def _silu(x):
    return jax.nn.silu(x)

def _sigmoid(x):
    return jax.nn.sigmoid(x)

def _layernorm(x, axis=-1, eps=1e-05):
    m = jnp.mean(x, axis=axis, keepdims=True)
    v = jnp.var(x, axis=axis, keepdims=True)
    return (x - m) / jnp.sqrt(v + eps)

def _scatter_add(tgt, idx, src, axis=0):
    return tgt.at[idx].add(src)

def _segment_sum(src, seg, n):
    return jax.ops.segment_sum(src, seg, n)
kernel_name = 'mk_prb_d1_jaxref_r4_1840f5'

def setup_inputs(seed: int=0):
    np.random.seed(seed)
    _w = jnp.asarray

    def _L0_attn_setup():
        import math
        import jax, jax.numpy as jnp
        import numpy as np
        EMBED_DIM = 256
        NUM_HEADS = 16
        HEAD_DIM = EMBED_DIM // NUM_HEADS
        NUM_BUCKETS = 32
        MAX_DISTANCE = 128

        def _relative_position_bucket(relative_position, num_buckets=NUM_BUCKETS, max_distance=MAX_DISTANCE):
            num_buckets = num_buckets // 2
            relative_buckets = (relative_position > 0).astype(jnp.int32) * num_buckets
            relative_position = jnp.abs(relative_position)
            max_exact = num_buckets // 2
            is_small = relative_position < max_exact
            rp_large = jnp.log(relative_position.astype(jnp.float32) / max_exact) / math.log(max_distance / max_exact)
            rp_large = max_exact + (rp_large * (num_buckets - max_exact)).astype(jnp.int32)
            rp_large = jnp.minimum(rp_large, num_buckets - 1)
            relative_buckets = relative_buckets + jnp.where(is_small, relative_position, rp_large)
            return relative_buckets

        def compute_bias(rel_emb, query_length, key_length):
            context_position = jnp.arange(query_length, dtype=jnp.int32)[:, None]
            memory_position = jnp.arange(key_length, dtype=jnp.int32)[None, :]
            relative_position = memory_position - context_position
            buckets = _relative_position_bucket(relative_position)
            values = rel_emb[buckets]
            return jnp.transpose(values, (2, 0, 1))[None]
        key = jax.random.key(seed)
        k1, k2, k3, k4 = jax.random.split(key, 4)
        B, S = (2, 512)
        hidden_states = jax.random.normal(k1, (B, S, EMBED_DIM), dtype=jnp.float32)
        scale = 1.0 / math.sqrt(EMBED_DIM)
        W_qkv = jax.random.normal(k2, (EMBED_DIM, 3 * EMBED_DIM), dtype=jnp.float32) * scale
        W_out = jax.random.normal(k3, (EMBED_DIM, EMBED_DIM), dtype=jnp.float32) * scale
        rel_emb = jax.random.normal(k4, (NUM_BUCKETS, NUM_HEADS), dtype=jnp.float32) * 0.02
        return {'hidden_states': hidden_states, 'W_qkv': W_qkv, 'W_out': W_out, 'rel_emb': rel_emb}
    _L0_attn_in = _L0_attn_setup()

    def _L0_ffn_setup():
        import jax, jax.numpy as jnp
        import numpy as np
        NUM_EXPERTS = 8
        TOP_K = 2
        key = jax.random.key(seed)
        ks = jax.random.split(key, 4)
        B, S, H, F = (4, 1024, 256, 1024)
        x = jax.random.normal(ks[0], (B, S, H), dtype=jnp.float32)
        router_w = jax.random.normal(ks[1], (H, NUM_EXPERTS), dtype=jnp.float32) * 0.02
        w1 = jax.random.normal(ks[2], (H, F), dtype=jnp.float32) * 0.02
        b1 = jnp.zeros((F,), dtype=jnp.float32)
        w2 = jax.random.normal(ks[3], (F, H), dtype=jnp.float32) * 0.02
        b2 = jnp.zeros((H,), dtype=jnp.float32)
        return {'x': x, 'router_w': router_w, 'w1': w1, 'b1': b1, 'w2': w2, 'b2': b2}
    _L0_ffn_in = _L0_ffn_setup()
    _d = {'L0_attn_hidden_states': _L0_attn_in['hidden_states'], 'L0_attn_W_qkv': _L0_attn_in['W_qkv'], 'L0_attn_W_out': _L0_attn_in['W_out'], 'L0_attn_rel_emb': _L0_attn_in['rel_emb'], 'L0_ffn_router_w': _L0_ffn_in['router_w'], 'L0_ffn_w1': _L0_ffn_in['w1'], 'L0_ffn_b1': _L0_ffn_in['b1'], 'L0_ffn_w2': _L0_ffn_in['w2'], 'L0_ffn_b2': _L0_ffn_in['b2']}
    _x0 = _d['L0_attn_hidden_states']
    _d['L0_attn_hidden_states'] = jax.random.normal(jax.random.fold_in(jax.random.key(seed), 1), (4, 2048, 256), dtype=_x0.dtype)
    del _x0
    return _d

def reference(L0_attn_hidden_states, L0_attn_W_qkv, L0_attn_W_out, L0_attn_rel_emb, L0_ffn_router_w, L0_ffn_w1, L0_ffn_b1, L0_ffn_w2, L0_ffn_b2):

    def _L0_attn_ref(hidden_states, W_qkv, W_out, rel_emb):
        import math
        import jax, jax.numpy as jnp
        import numpy as np
        EMBED_DIM = 256
        NUM_HEADS = 16
        HEAD_DIM = EMBED_DIM // NUM_HEADS
        NUM_BUCKETS = 32
        MAX_DISTANCE = 128

        def _relative_position_bucket(relative_position, num_buckets=NUM_BUCKETS, max_distance=MAX_DISTANCE):
            num_buckets = num_buckets // 2
            relative_buckets = (relative_position > 0).astype(jnp.int32) * num_buckets
            relative_position = jnp.abs(relative_position)
            max_exact = num_buckets // 2
            is_small = relative_position < max_exact
            rp_large = jnp.log(relative_position.astype(jnp.float32) / max_exact) / math.log(max_distance / max_exact)
            rp_large = max_exact + (rp_large * (num_buckets - max_exact)).astype(jnp.int32)
            rp_large = jnp.minimum(rp_large, num_buckets - 1)
            relative_buckets = relative_buckets + jnp.where(is_small, relative_position, rp_large)
            return relative_buckets

        def compute_bias(rel_emb, query_length, key_length):
            context_position = jnp.arange(query_length, dtype=jnp.int32)[:, None]
            memory_position = jnp.arange(key_length, dtype=jnp.int32)[None, :]
            relative_position = memory_position - context_position
            buckets = _relative_position_bucket(relative_position)
            values = rel_emb[buckets]
            return jnp.transpose(values, (2, 0, 1))[None]
        B, S, _ = hidden_states.shape
        qkv = hidden_states @ W_qkv
        qkv = qkv.reshape(B, S, 3, NUM_HEADS, HEAD_DIM)
        qkv = jnp.transpose(qkv, (0, 3, 2, 1, 4))
        q, k, v = (qkv[:, :, 0], qkv[:, :, 1], qkv[:, :, 2])
        scores = jnp.einsum('bhqd,bhkd->bhqk', q, k)
        scores = scores + compute_bias(rel_emb, S, S)
        attn = jax.nn.softmax(scores.astype(jnp.float32), axis=-1).astype(scores.dtype)
        out = jnp.einsum('bhqk,bhkd->bhqd', attn, v)
        out = jnp.transpose(out, (0, 2, 1, 3)).reshape(B, S, EMBED_DIM)
        return out @ W_out

    def _L0_ffn_ref(x, router_w, w1, b1, w2, b2):
        import jax, jax.numpy as jnp
        import numpy as np
        NUM_EXPERTS = 8
        TOP_K = 2
        B, S, H = x.shape
        xt = x.reshape(-1, H)
        router_logits = jnp.matmul(xt, router_w)
        router_probs = jax.nn.softmax(router_logits, axis=-1)
        top_k_probs, top_k_indices = jax.lax.top_k(router_probs, TOP_K)
        top_k_probs = top_k_probs / jnp.sum(top_k_probs, axis=-1, keepdims=True)
        one_hot = jax.nn.one_hot(top_k_indices, NUM_EXPERTS, dtype=xt.dtype)
        combine = jnp.einsum('tk,tke->te', top_k_probs, one_hot)
        expert_out = jnp.matmul(jax.nn.gelu(jnp.matmul(xt, w1) + b1), w2) + b2
        out = expert_out * jnp.sum(combine, axis=-1, keepdims=True)
        return out.reshape(B, S, H)
    x = L0_attn_hidden_states
    xn = _layernorm(x, axis=-1)
    x = x + _L0_attn_ref(xn, L0_attn_W_qkv, L0_attn_W_out, L0_attn_rel_emb) + _L0_ffn_ref(xn, L0_ffn_router_w, L0_ffn_w1, L0_ffn_b1, L0_ffn_w2, L0_ffn_b2)
    return x

_drawn_inputs = setup_inputs


def setup_inputs(seed=0):
    import zlib

    import numpy as np

    out = dict(_drawn_inputs(seed))
    spreads = {'L0_ffn_b1': (0.0, 0.1), 'L0_ffn_b2': (0.0, 0.1)}
    factors = {'L0_attn_rel_emb': 8.0, 'L0_ffn_router_w': 8.0}
    for name, (base, spread) in spreads.items():
        noise = np.random.default_rng([zlib.crc32(name.encode()), seed]).standard_normal(out[name].shape)
        drawn = base * np.exp(spread * noise) if base else spread * noise
        out[name] = jnp.asarray(drawn.astype(out[name].dtype))
    for name, factor in factors.items():
        out[name] = (out[name] * factor).astype(out[name].dtype)
    return out
```

```python
import concourse.bass as bass
from concourse import mybir
from contextlib import ExitStack

F32 = mybir.dt.float32
BF16 = mybir.dt.bfloat16
ALU = mybir.AluOpType
ACT = mybir.ActivationFunctionType
AX = mybir.AxisListType

B, S, E = 4, 2048, 256
H, D = 16, 16
F = 1024
NX = 8
P = 128
CH = 512
KE = E // P
KF = F // P
TPC = CH // P
CPB = S // CH
KB = S // P
NH = B * H
TILES = B * KB
EPS = 1e-5

BUCKETS = 32
NEAR = 96
NQ = P + 2 * NEAR
LINE = NQ + P

PARTS = 3
PAIRS = 6
ROWS = PAIRS * D
GROUP = 4
GROUPS = NH // GROUP
LEAD = 4


def bucket_line():
    import numpy as np

    half = BUCKETS // 2
    exact = half // 2
    firsts = [next(n for n in range(exact, 200) if n * n >= exact * exact * 2**j) for j in range(half - exact)]
    hot = np.zeros((BUCKETS, LINE), np.float32)
    for x in range(LINE):
        rel = P + NEAR - 1 - x
        n = abs(rel)
        bucket = n if n < exact else exact - 1 + sum(n >= f for f in firsts)
        hot[bucket + (half if rel > 0 else 0), x] = 1.0
    return hot


def wait(eng, sem, value):
    if not isinstance(value, int) or value > 0:
        eng.wait_ge(sem, value)


def transformer_layer(nc, x, w_qkv, w_out, rel_emb, router_w, w1, b1, w2, b2, hot, out):
    qk_d = nc.dram_tensor("qk_parts", [2, PARTS, NH * D, S], BF16).ap()
    line_d = nc.dram_tensor("bias_line", [H, LINE], F32).ap()
    near_d = nc.dram_tensor("bias_near", [NH, P, NQ], F32).ap()
    ffn_d = nc.dram_tensor("ffn_rows", [B * S, E], F32).ap()

    ctx = ExitStack()
    with ctx:
        def sb(name, shape, dt=F32, c=ctx):
            return c.enter_context(nc.sbuf_tensor(name, shape, dt))

        def sem(name):
            return ctx.enter_context(nc.semaphore(name))

        ps = ctx.enter_context(nc.psum_tensor("ps", [P, 8, CH], F32))
        ident = sb("ident", [P, P])
        v_all = sb("v_all", [P, NH, KB, D])
        logits = sb("logits", [P, TILES, NX])

        c1 = ExitStack()
        with c1:
            w_qk_sb = sb("w_qk_sb", [P, KE, 2 * E], c=c1)
            w_vr_sb = sb("w_vr_sb", [P, KE, E + NX], c=c1)
            w1_sb = sb("w1_sb", [P, KE, F], c=c1)
            w2_sb = sb("w2_sb", [P, KF, E], c=c1)
            b1_sb = sb("b1_sb", [P, KF], c=c1)
            b2_sb = sb("b2_sb", [P, E], c=c1)
            emb_sb = sb("emb_sb", [BUCKETS, H], c=c1)
            hot_sb = sb("hot_sb", [BUCKETS, LINE], c=c1)
            line_sb = sb("line_sb", [H, LINE], c=c1)
            line_exp = sb("line_exp", [H, LINE], c=c1)
            power = sb("power", [P, TPC], c=c1)
            x_sb = sb("x_sb", [P, 2, TPC, E], c=c1)
            stats = sb("stats", [P, TPC, 6], c=c1)
            mean_var = sb("mean_var", [P, TPC, 2], c=c1)
            var_eps = sb("var_eps", [P, TPC], c=c1)
            rstd = sb("rstd", [P, TPC], c=c1)
            xn = sb("xn", [P, TPC, E], c=c1)
            xnt = sb("xnt", [P, 2, KE, CH], c=c1)
            parts = sb("parts", [P, 2, PARTS, CH], BF16, c=c1)
            rest = sb("rest", [P, 2, CH], c=c1)
            hid = sb("hid", [P, KF, CH], c=c1)
            ffn_sb = sb("ffn_sb", [P, 2, TPC, E], c=c1)

            w_loaded = sem("w_loaded")
            line_in = sem("line_in")
            ident_zeroed = sem("ident_zeroed")
            ident_made = sem("ident_made")
            line_mm = sem("line_mm")
            line_shifted = sem("line_shifted")
            line_ready = sem("line_ready")
            line_stored = sem("line_stored")
            near_stored = sem("near_stored")
            x_loaded = [sem(f"x_loaded{i}") for i in range(2)]
            stats_done = sem("stats_done")
            aggr_done = sem("aggr_done")
            var_done = sem("var_done")
            rstd_done = sem("rstd_done")
            xn_done = sem("xn_done")
            xt_ready = sem("xt_ready")
            xt_copied_a = sem("xt_copied_a")
            xt_copied_v = sem("xt_copied_v")
            qk_ready = sem("qk_ready")
            hi_done = sem("hi_done")
            rest_done = sem("rest_done")
            mid_done = sem("mid_done")
            lo_done = sem("lo_done")
            parts_stored = [sem(f"parts_stored{i}") for i in range(2)]
            vr_ready = sem("vr_ready")
            v_copied = sem("v_copied")
            r_copied = sem("r_copied")
            f1_ready = sem("f1_ready")
            gelu_done = sem("gelu_done")
            f2_ready = sem("f2_ready")
            f2_copied = sem("f2_copied")
            ffn_stored = [sem(f"ffn_stored{i}") for i in range(2)]
            W_LOADS = 7

            block = c1.enter_context(nc.Block())

            @block.sync
            def _(sp):
                sp.dma_start(emb_sb[:], rel_emb).then_inc(line_in, 16)
                sp.dma_start(hot_sb[:], hot).then_inc(line_in, 16)

                def load_x(b, c):
                    wait(sp, xn_done, CPB * b + c - 1)
                    sp.dma_start(x_sb[:, c % 2], x[bass.ds(S * (b % B) + CH * c, CH), :].rearrange("(t p) e -> p t e", p=P)) \
                        .then_inc(x_loaded[c % 2], 16)

                load_x(0, 0)
                load_x(0, 1)
                sp.dma_start(w_qk_sb[:], w_qkv[:, 0:2 * E].rearrange("(k p) n -> p k n", p=P)).then_inc(w_loaded, 16)
                sp.dma_start(w_vr_sb[:, :, 0:E], w_qkv[:, 2 * E:3 * E].rearrange("(k p) n -> p k n", p=P)).then_inc(w_loaded, 16)
                sp.dma_start(w_vr_sb[:, :, E:E + NX], router_w.rearrange("(k p) n -> p k n", p=P)).then_inc(w_loaded, 16)
                sp.dma_start(w1_sb[:], w1.rearrange("(k p) n -> p k n", p=P)).then_inc(w_loaded, 16)
                sp.dma_start(w2_sb[:], w2.rearrange("(k p) n -> p k n", p=P)).then_inc(w_loaded, 16)
                sp.dma_start(b1_sb[:], b1.rearrange("(k p) -> p k", p=P), allow_slow_non_contiguous=True).then_inc(w_loaded, 16)
                sp.dma_start(b2_sb[:], bass.AP(tensor=b2.tensor, offset=0, ap=[[0, P], [1, E]])).then_inc(w_loaded, 16)

                sp.wait_ge(line_ready, 1)
                sp.dma_start(line_d, line_exp[:]).then_inc(line_stored, 16)
                sp.wait_ge(line_stored, 16)
                for b in range(B):
                    sp.dma_start(near_d[H * b:H * (b + 1)],
                                 bass.AP(tensor=line_d.tensor, offset=P - 1, ap=[[LINE, H], [-1, P], [1, NQ]])) \
                        .then_inc(near_stored, 16)

                def chunk(b, c):
                    for m in range(2 * KE):
                        wait(sp, lo_done, 2 * KE * (CPB * b + c) + m + 1)
                        sp.dma_start(qk_d[m // KE, :, bass.ds(E * b + P * (m % KE), P), CH * c:CH * (c + 1)].rearrange("s r n -> r s n"),
                                     parts[:, m % 2]).then_inc(parts_stored[m % 2], 16)
                    wait(sp, f2_copied, TPC * (CPB * b + c + 1))
                    sp.dma_start(ffn_d[bass.ds(S * b + CH * c, CH), :].rearrange("(t p) e -> p t e", p=P), ffn_sb[:, c % 2]) \
                        .then_inc(ffn_stored[c % 2], 16)

                def batch(b):
                    for c in range(CPB):
                        if c + 2 < CPB:
                            load_x(b, c + 2)
                        else:
                            load_x(b + 1, c + 2 - CPB)
                        chunk(b, c)

                batch(0)
                with sp.Fori(1, B) as b:
                    batch(b)
                sp.wait_ge(x_loaded[0], 16 * (CPB // 2 * B + 1))
                sp.wait_ge(x_loaded[1], 16 * (CPB // 2 * B + 1))
                sp.wait_ge(near_stored, 16 * B)
                for i in range(2):
                    sp.wait_ge(parts_stored[i], 16 * KE * CPB * B)
                    sp.wait_ge(ffn_stored[i], 16 * CPB // 2 * B)

            @block.gpsimd
            def _(pool):
                nc.gpsimd.memset(ident[:], 0.0).then_inc(ident_zeroed, 1)
                pool.wait_ge(ident_zeroed, 1)
                nc.gpsimd.affine_select(out=ident[:], in_=ident[:], compare_op=ALU.not_equal, fill=1.0, base=0,
                                        pattern=[[-1, P]], channel_multiplier=1).then_inc(ident_made, 1)
                nc.gpsimd.memset(power[:], -0.5).then_inc(ident_made, 1)
                pool.wait_ge(ident_made, 2)

                def norm(n):
                    wait(pool, var_done, n + 1)
                    wait(pool, xn_done, n)
                    nc.gpsimd.tensor_tensor(rstd[:], var_eps[:], power[:], ALU.pow).then_inc(rstd_done, 1)

                def chunk(n):
                    for m in range(2 * KE):
                        i = 2 * KE * n + m
                        wait(pool, mid_done, i + 1)
                        nc.gpsimd.tensor_tensor(parts[:, m % 2, 2], rest[:, m % 2], parts[:, m % 2, 1], ALU.subtract) \
                            .then_inc(lo_done, 1)

                def batch(b):
                    for c in range(CPB):
                        norm(CPB * b + c + 1)
                        chunk(CPB * b + c)

                norm(0)
                batch(0)
                with pool.Fori(1, B) as b:
                    batch(b)

            @block.vector
            def _(dve):
                dve.wait_ge(line_mm, 1)
                nc.vector.tensor_scalar(line_sb[:], ps[0:H, 7, 0:LINE], ps[0:H, 7, LINE - 1:LINE], None, ALU.subtract) \
                    .then_inc(line_shifted, 1)

                def norm_stats(b, c):
                    n = CPB * b + c
                    wait(dve, x_loaded[c % 2], 16 * (CPB // 2 * b + c // 2 + 1))
                    for t in range(TPC):
                        last = nc.vector.bn_stats(stats[:, t], x_sb[:, c % 2, t])
                    last.then_inc(stats_done, 1)
                    wait(dve, stats_done, n + 1)

                def norm_var(n):
                    for t in range(TPC):
                        last = nc.vector.bn_aggr(mean_var[:, t], stats[:, t])
                    last.then_inc(aggr_done, 1)
                    wait(dve, aggr_done, n + 1)
                    nc.vector.tensor_scalar(var_eps[:], mean_var[:, :, 1], EPS, None, ALU.add).then_inc(var_done, 1)

                def scale(b, c):
                    n = CPB * b + c
                    wait(dve, rstd_done, n + 1)
                    wait(dve, xt_ready, n)
                    for t in range(TPC):
                        last = nc.vector.tensor_scalar(xn[:, t], x_sb[:, c % 2, t], mean_var[:, t, 0:1], rstd[:, t:t + 1],
                                                       ALU.subtract, ALU.mult)
                    last.then_inc(xn_done, 1)

                def chunk(b, c):
                    n = CPB * b + c
                    nb, ncc = (b, c + 1) if c + 1 < CPB else (b + 1, 0)
                    wait(dve, xt_ready, n + 1)
                    wait(dve, f1_ready, KF * (n - 1))
                    nc.vector.tensor_copy(xnt[:, c % 2, 1], ps[:, 1]).then_inc(xt_copied_v, 1)
                    norm_stats(nb, ncc)
                    for m in range(2 * KE):
                        i = 2 * KE * n + m
                        if m == 1:
                            norm_var(n + 1)
                        wait(dve, hi_done, i + 1)
                        wait(dve, lo_done, i - 1)
                        nc.vector.tensor_tensor(rest[:, m % 2], ps[:, 2 + m % 2], parts[:, m % 2, 0], ALU.subtract) \
                            .then_inc(rest_done, 1)
                    scale(nb, ncc)
                    for t in range(TPC):
                        wait(dve, f2_ready, TPC * n + t + 1)
                        if t == 0:
                            wait(dve, ffn_stored[c % 2], 16 * (CPB // 2 * b + c // 2))
                        nc.vector.tensor_tensor(ffn_sb[:, c % 2, t], ps[:, 6 + t // 2, E * (t % 2):E * (t % 2 + 1)], b2_sb[:],
                                                ALU.add).then_inc(f2_copied, 1)

                dve.wait_ge(w_loaded, 16 * W_LOADS)
                norm_stats(0, 0)
                norm_var(0)
                scale(0, 0)
                for c in range(CPB):
                    chunk(0, c)
                with dve.Fori(1, B) as b:
                    for c in range(CPB):
                        chunk(b, c)

            @block.scalar
            def _(act):
                act.wait_ge(line_shifted, 1)
                nc.scalar.activation(line_exp[:], line_sb[:], ACT.Exp).then_inc(line_ready, 1)
                act.wait_ge(w_loaded, 16 * W_LOADS)

                def chunk(b, c):
                    n = CPB * b + c
                    wait(act, xt_ready, n + 1)
                    wait(act, f1_ready, KF * (n - 1))
                    nc.scalar.activation(xnt[:, c % 2, 0], ps[:, 0], ACT.Copy).then_inc(xt_copied_a, 1)
                    for m in range(2 * KE + 1):
                        i = 2 * KE * n + m
                        if m < 2 * KE:
                            wait(act, qk_ready, i + 1)
                            wait(act, parts_stored[m % 2], 16 * (KE * n + m // 2))
                            nc.scalar.activation(parts[:, m % 2, 0], ps[:, 2 + m % 2], ACT.Copy).then_inc(hi_done, 1)
                        if m > 0:
                            wait(act, rest_done, i)
                            nc.scalar.activation(parts[:, (m - 1) % 2, 1], rest[:, (m - 1) % 2], ACT.Copy).then_inc(mid_done, 1)
                    for t in range(TPC):
                        wait(act, vr_ready, TPC * n + t + 1)
                        nc.scalar.activation(v_all[:, bass.ds(H * b, H), TPC * c + t, :],
                                             ps[:, 2 + t % 2, 0:E].rearrange("p (h d) -> p h d", d=D), ACT.Copy) \
                            .then_inc(v_copied, 1)
                        nc.scalar.activation(logits[:, bass.ds(KB * b + TPC * c + t, 1), :].rearrange("p a n -> p (a n)"),
                                             ps[:, 2 + t % 2, E:E + NX], ACT.Copy).then_inc(r_copied, 1)
                    for f in range(KF):
                        wait(act, f1_ready, KF * n + f + 1)
                        if f == 0:
                            wait(act, f2_ready, TPC * n)
                        nc.scalar.activation(hid[:, f], ps[:, 4 + f % 2], ACT.Gelu_apprx_tanh, bias=b1_sb[:, f:f + 1]) \
                            .then_inc(gelu_done, 1)

                for c in range(CPB):
                    chunk(0, c)
                with act.Fori(1, B) as b:
                    for c in range(CPB):
                        chunk(b, c)

            @block.tensor
            def _(pe):
                pe.wait_ge(line_in, 32)
                nc.tensor.matmul(ps[0:H, 7, 0:LINE], emb_sb[:], hot_sb[:], start=True, stop=True).then_inc(line_mm, 1)
                pe.wait_ge(ident_made, 2)
                pe.wait_ge(w_loaded, 16 * W_LOADS)
                pe.wait_ge(line_shifted, 1)

                def transposes(n):
                    wait(pe, xn_done, n + 1)
                    wait(pe, xt_copied_a, n)
                    wait(pe, xt_copied_v, n)
                    for t in range(TPC):
                        for k in range(KE):
                            last = nc.tensor.transpose(ps[:, k, P * t:P * (t + 1)], xn[:, t, P * k:P * (k + 1)], ident[:])
                    last.then_inc(xt_ready, 1)

                def chunk(b, c):
                    n = CPB * b + c
                    xt = xnt[:, c % 2]
                    wait(pe, xt_copied_a, n + 1)
                    wait(pe, xt_copied_v, n + 1)
                    for m in range(2 * KE):
                        if m < 2:
                            wait(pe, v_copied, TPC * n - 1 + m)
                            wait(pe, r_copied, TPC * n - 1 + m)
                        else:
                            wait(pe, rest_done, 2 * KE * n + m - 1)
                        for k in range(KE):
                            last = nc.tensor.matmul(ps[:, 2 + m % 2], w_qk_sb[:, k, P * m:P * (m + 1)], xt[:, k],
                                                    start=k == 0, stop=k == KE - 1)
                        last.then_inc(qk_ready, 1)
                    for t in range(TPC):
                        if t < 2:
                            wait(pe, rest_done, 2 * KE * (n + 1) - 1 + t)
                        else:
                            wait(pe, v_copied, TPC * n + t - 1)
                            wait(pe, r_copied, TPC * n + t - 1)
                        for k in range(KE):
                            last = nc.tensor.matmul(ps[:, 2 + t % 2, 0:E + NX], xt[:, k, P * t:P * (t + 1)], w_vr_sb[:, k],
                                                    start=k == 0, stop=k == KE - 1)
                        last.then_inc(vr_ready, 1)
                    for f in range(KF):
                        wait(pe, gelu_done, KF * n + f - 1)
                        for k in range(KE):
                            last = nc.tensor.matmul(ps[:, 4 + f % 2], w1_sb[:, k, P * f:P * (f + 1)], xt[:, k],
                                                    start=k == 0, stop=k == KE - 1)
                        last.then_inc(f1_ready, 1)
                    transposes(n + 1)
                    wait(pe, gelu_done, KF * (n + 1))
                    for t in range(TPC):
                        wait(pe, f2_copied, TPC * n + (t // 2) * 2 - 2 if t % 2 == 0 else TPC * n + t)
                        for f in range(KF):
                            last = nc.tensor.matmul(ps[:, 6 + t // 2, E * (t % 2):E * (t % 2 + 1)], hid[:, f, P * t:P * (t + 1)],
                                                    w2_sb[:, f], start=f == 0, stop=f == KF - 1)
                        last.then_inc(f2_ready, 1)

                transposes(0)
                for c in range(CPB):
                    chunk(0, c)
                with pe.Fori(1, B) as b:
                    for c in range(CPB):
                        chunk(b, c)

        c2 = ExitStack()
        with c2:
            q_st = [sb(f"q_st{u}", [ROWS + 1, S], BF16, c=c2) for u in range(GROUP)]
            k_st = [sb(f"k_st{u}", [ROWS + 1, S], BF16, c=c2) for u in range(GROUP)]
            near = [sb(f"near{u}", [P, NQ], c=c2) for u in range(GROUP)]
            vx = sb("vx", [P, 2, KB, 32], c=c2)
            vr = sb("vr", [P, 2, KB, 32], c=c2)
            prob = sb("prob", [P, 2, S], c=c2)
            max_half = sb("max_half", [P, 2, KB, 2], c=c2)
            max_neg = sb("max_neg", [P, 2, KB], c=c2)
            shift_row = sb("shift_row", [KB, 2, P], BF16, c=c2)
            o_sb = sb("o_sb", [P, CH], c=c2)
            recip = sb("recip", [P, TPC, CPB], c=c2)

            stacks_in = [sem(f"stacks_in{u}") for u in range(GROUP)]
            shift_in = [sem(f"shift_in{u}") for u in range(GROUP)]
            near_in = [sem(f"near_in{u}") for u in range(GROUP)]
            ones_set = sem("ones_set")
            score_ready = sem("score_ready")
            exp_done = sem("exp_done")
            near_done = sem("near_done")
            pv_done = sem("pv_done")
            v_read = sem("v_read")
            v_built = sem("v_built")
            max_ready = sem("max_ready")
            max_done = sem("max_done")
            neg_done = sem("neg_done")
            shift_turned = sem("shift_turned")
            shift_copied = sem("shift_copied")
            o_copied = sem("o_copied")
            o_turned = sem("o_turned")
            recip_done = sem("recip_done")
            o_done = sem("o_done")

            STACK_LOADS = 2 * PAIRS
            Q_PART = [0, 0, 0, 1, 1, 2]
            K_PART = [0, 1, 2, 0, 1, 0]

            def near_span(kb):
                first = P * kb - NEAR
                return max(first, 0), min(first + NQ, S), max(-first, 0)

            def max_at(n, step):
                return (n + 1, step + LEAD) if step + LEAD < KB else (n + 2, step + LEAD - KB)

            block = c2.enter_context(nc.Block())

            @block.sync
            def _(sp):
                def load(n, u):
                    wait(sp, score_ready, CPB * KB * (n - GROUP + 1))
                    for i in range(PAIRS):
                        sp.dma_start(q_st[u][D * i:D * (i + 1), :], qk_d[0, Q_PART[i], bass.ds(D * n, D), :]).then_inc(stacks_in[u], 16)
                        sp.dma_start(k_st[u][D * i:D * (i + 1), :], qk_d[1, K_PART[i], bass.ds(D * n, D), :]).then_inc(stacks_in[u], 16)
                    wait(sp, near_done, KB * (n - GROUP + 1))
                    sp.dma_start(near[u][:], near_d[bass.ds(n, 1)].rearrange("a p c -> (a p) c")).then_inc(near_in[u], 16)

                def shift(n, u):
                    wait(sp, shift_copied, n + 1)
                    sp.dma_start(q_st[u][ROWS:ROWS + 1, :].rearrange("a (i p) -> a i p", p=P), shift_row[:, n % 2 if isinstance(n, int) else u % 2, :]) \
                        .then_inc(shift_in[u], 16)

                def group(g, last=False):
                    for u in range(GROUP):
                        n = GROUP * g + u
                        if not (last and u > 0):
                            load(n + 3, (u + 3) % GROUP)
                        if not (last and u == GROUP - 1):
                            shift(n + 1, (u + 1) % GROUP)

                for u in range(3):
                    load(u, u)
                shift(0, 0)
                group(0)
                with sp.Fori(1, GROUPS - 1) as g:
                    group(g)
                group(GROUPS - 1, last=True)

            @block.scalar
            def _(act):
                def shift(n, par):
                    wait(act, shift_turned, n + 1)
                    nc.scalar.activation(shift_row[:, par % 2, :], ps[0:KB, 6 + par % 2, 0:P], ACT.Copy).then_inc(shift_copied, 1)

                def head(n, u, last=False):
                    for kb in range(KB):
                        if kb == 13 and not last:
                            shift(n + 1, (u + 1) % GROUP)
                        for c in range(CPB):
                            i = CPB * (KB * n + kb) + c
                            wait(act, score_ready, i + 1)
                            wait(act, pv_done, i - 2 * CPB + 1)
                            nc.scalar.activation(prob[:, kb % 2, CH * c:CH * (c + 1)], ps[:, c % 2], ACT.Exp).then_inc(exp_done, 1)

                shift(0, 0)
                for u in range(GROUP):
                    head(u, u)
                with act.Fori(1, GROUPS - 1) as g:
                    for u in range(GROUP):
                        head(GROUP * g + u, u)
                for u in range(GROUP):
                    head(NH - GROUP + u, u, last=u == GROUP - 1)

            @block.gpsimd
            def _(pool):
                def build(n, u, turn):
                    wait(pool, pv_done, CPB * KB * (n - 1))
                    pool.wait_ge(ones_set, GROUP + 2)
                    nc.gpsimd.tensor_copy(vx[:, u % 2, :, 0:D], v_all[:, bass.ds(n, 1)].rearrange("p a k d -> p (a k) d")) \
                        .then_inc(v_read, 1)
                    pool.wait_ge(near_in[u], 16 * turn)
                    wait(pool, v_read, n + 1)
                    nc.gpsimd.tensor_tensor(vr[:, u % 2], vx[:, u % 2],
                                            near[u][:, 0:1].unsqueeze(2).to_broadcast([P, KB, 32]), ALU.mult).then_inc(v_built, 1)

                def head(g, u, last=False):
                    n = GROUP * g + u
                    for kb in range(KB):
                        if kb == 4 and not last:
                            build(n + 1, (u + 1) % GROUP, g + 1 if u + 1 < GROUP else g + 2)
                        q0, q1, c0 = near_span(kb)
                        wait(pool, exp_done, CPB * (KB * n + kb) + (q1 - 1) // CH + 1)
                        nc.gpsimd.tensor_tensor(prob[:, kb % 2, q0:q1], prob[:, kb % 2, q0:q1], near[u][:, c0:c0 + q1 - q0],
                                                ALU.mult).then_inc(near_done, 1)

                build(0, 0, 1)
                for u in range(GROUP):
                    head(0, u)
                with pool.Fori(1, GROUPS - 1) as g:
                    for u in range(GROUP):
                        head(g, u)
                for u in range(GROUP):
                    head(GROUPS - 1, u, last=u == GROUP - 1)

            @block.vector
            def _(dve):
                def maxima(m, par, i):
                    for half in range(2):
                        wait(dve, max_ready, 2 * (KB * m + i) + half + 1)
                        if i == 0 and half == 0:
                            wait(dve, neg_done, m - 1)
                        nc.vector.reduce_max(max_half[:, par % 2, i, half:half + 1],
                                             ps[:, 2 + 2 * half:4 + 2 * half].rearrange("p a n -> p (a n)"), AX.X).then_inc(max_done, 1)

                def combine(m, par):
                    wait(dve, max_done, 2 * KB * (m + 1))
                    wait(dve, shift_turned, m - 1)
                    nc.vector.tensor_reduce(max_neg[:, par % 2], max_half[:, par % 2], AX.X, ALU.max, negate=True).then_inc(neg_done, 1)

                def collect(n, par):
                    wait(dve, pv_done, CPB * KB * (n + 1))
                    wait(dve, o_turned, n)
                    nc.vector.tensor_copy(o_sb[:], ps[:, 6 + par % 2]).then_inc(o_copied, 1)

                def normalise(n, par):
                    turned = ps[:, 6 + par % 2].rearrange("p (i c w) -> p i c w", i=TPC, c=CPB)
                    wait(dve, o_turned, n + 1)
                    wait(dve, o_done, n)
                    nc.vector.reciprocal(recip[:], turned[:, :, :, D]).then_inc(recip_done, 1)
                    wait(dve, recip_done, n + 1)
                    wait(dve, v_read, n + 1)
                    for c in range(CPB):
                        last = nc.vector.tensor_tensor(
                            v_all[:, bass.ds(n, 1), TPC * c:TPC * (c + 1), :].rearrange("p a i d -> p (a i) d"),
                            turned[:, :, c, 0:D], recip[:, :, c:c + 1].to_broadcast([P, TPC, D]), ALU.mult)
                    last.then_inc(o_done, 1)

                def head(n, u, first=False, left=2):
                    for kb in range(KB):
                        ahead = 1 if kb + LEAD < KB else 2
                        m, i = max_at(n, kb)
                        if ahead <= left:
                            maxima(m, (u + ahead) % 2, i)
                        if kb == 0 and not first:
                            collect(n - 1, u + 1)
                        if kb == 2 and not first:
                            normalise(n - 1, u + 1)
                        if kb == KB - 1 - LEAD and left >= 1:
                            combine(n + 1, u + 1)

                for u in range(GROUP):
                    nc.vector.memset(k_st[u][ROWS:ROWS + 1, :], 1.0).then_inc(ones_set, 1)
                nc.vector.memset(vx[:, :, :, D + 1:32], 0.0).then_inc(ones_set, 1)
                nc.vector.memset(vx[:, :, :, D:D + 1], 1.0).then_inc(ones_set, 1)
                for i in range(KB):
                    maxima(0, 0, i)
                combine(0, 0)
                for i in range(LEAD):
                    maxima(1, 1, i)
                for u in range(GROUP):
                    head(u, u, first=u == 0)
                with dve.Fori(1, GROUPS - 1) as g:
                    for u in range(GROUP):
                        head(GROUP * g + u, u)
                for u in range(GROUP):
                    head(NH - GROUP + u, u, left=GROUP - 1 - u)
                collect(NH - 1, NH - 1)
                normalise(NH - 1, NH - 1)

            @block.tensor
            def _(pe):
                pe.wait_ge(ones_set, GROUP + 2)

                def maxima(m, u, i, c):
                    if c % 2 == 0:
                        wait(pe, max_done, 2 * (KB * m + i) + c // 2 - 1)
                    mm = nc.tensor.matmul(ps[:, 2 + c], q_st[u][0:ROWS, P * i:P * (i + 1)], k_st[u][0:ROWS, CH * c:CH * (c + 1)],
                                          start=True, stop=True)
                    if c % 2 == 1:
                        mm.then_inc(max_ready, 1)

                def turn_shift(m, par):
                    wait(pe, neg_done, m + 1)
                    wait(pe, o_done, m - 1)
                    nc.tensor.transpose(ps[0:KB, 6 + par % 2, 0:P], max_neg[:, par % 2], ident[:]).then_inc(shift_turned, 1)

                def scores(n, u, kb, c):
                    i = CPB * (KB * n + kb) + c
                    wait(pe, exp_done, i - 1)
                    nc.tensor.matmul(ps[:, c % 2], k_st[u][:, P * kb:P * (kb + 1)], q_st[u][:, CH * c:CH * (c + 1)],
                                     start=True, stop=True).then_inc(score_ready, 1)

                def values(n, u, kb, c):
                    q0, q1, _ = near_span(kb)
                    lo, hi = CH * c, CH * (c + 1)
                    if q0 < hi and q1 > lo:
                        wait(pe, near_done, KB * n + kb + 1)
                    else:
                        wait(pe, exp_done, CPB * (KB * n + kb) + c + 1)
                    if kb == 0 and c == 0:
                        wait(pe, v_built, n + 1)
                        wait(pe, shift_copied, n + 1)
                    cut = min(max(P * kb - NEAR, lo), hi)
                    for v, a, z in ((vr, lo, cut), (vx, cut, hi)):
                        if a < z:
                            last = nc.tensor.matmul(ps[32 * c:32 * (c + 1), 6 + u % 2, a - lo:z - lo], v[:, u % 2, kb],
                                                    prob[:, kb % 2, a:z], start=kb == 0, stop=kb == KB - 1 and z == hi)
                    last.then_inc(pv_done, 1)

                def turn_result(n, par):
                    wait(pe, o_copied, n + 1)
                    for i in range(TPC):
                        last = nc.tensor.transpose(ps[:, 6 + par % 2, P * i:P * (i + 1)], o_sb[:, P * i:P * (i + 1)], ident[:])
                    last.then_inc(o_turned, 1)

                def head(g, u, first=False, left=2):
                    n = GROUP * g + u
                    for kb in range(KB):
                        if kb == 2 and not first:
                            turn_result(n - 1, u + 1)
                        if kb == 13 and left >= 1:
                            turn_shift(n + 1, u + 1)
                        if kb == 0:
                            pe.wait_ge(shift_in[u], 16 * (g + 1))
                        ahead = 1 if kb + LEAD < KB else 2
                        m, i = max_at(n, kb)
                        mu = (u + ahead) % GROUP
                        if i == 0 and ahead <= left:
                            pe.wait_ge(stacks_in[mu], 16 * STACK_LOADS * (g + 1 + (u + ahead) // GROUP))
                        for c in range(CPB):
                            scores(n, u, kb, c)
                            if ahead <= left:
                                maxima(m, mu, i, c)
                            if kb > 0:
                                values(n, u, kb - 1, c)
                            elif not first:
                                values(n - 1, u + 1, KB - 1, c)

                for m in range(2):
                    pe.wait_ge(stacks_in[m], 16 * STACK_LOADS)
                    for i in range(KB if m == 0 else LEAD):
                        for c in range(CPB):
                            maxima(m, m, i, c)
                    if m == 0:
                        turn_shift(0, 0)
                for u in range(GROUP):
                    head(0, u, first=u == 0)
                with pe.Fori(1, GROUPS - 1) as g:
                    for u in range(GROUP):
                        head(g, u)
                for u in range(GROUP):
                    head(GROUPS - 1, u, left=GROUP - 1 - u)
                for c in range(CPB):
                    values(NH - 1, NH - 1, KB - 1, c)
                turn_result(NH - 1, NH - 1)

        c3 = ExitStack()
        with c3:
            wo_sb = sb("wo_sb", [P, KE, E], c=c3)
            top = sb("top", [P, TILES, NX], c=c3)
            top_x = sb("top_x", [P, TILES, NX], c=c3)
            total = sb("total", [P, TILES], c=c3)
            share = sb("share", [P, TILES, 2], c=c3)
            gate = sb("gate", [P, TILES], c=c3)
            xr = sb("xr", [P, 2, TPC, E], c=c3)
            yr = sb("yr", [P, 2, TPC, E], c=c3)
            res = sb("res", [P, 2, TPC, E], c=c3)
            rows = sb("rows", [P, 2, TPC, E], c=c3)
            turned = sb("turned", [P, 2, KE, CH], c=c3)

            wo_in = sem("wo_in")
            top_done = sem("top_done")
            top_exp = sem("top_exp")
            gate_step = sem("gate_step")
            rows_in = [sem(f"rows_in{i}") for i in range(2)]
            packed = sem("packed")
            a_turned = sem("a_turned")
            a_copied_a = sem("a_copied_a")
            a_copied_v = sem("a_copied_v")
            proj_ready = sem("proj_ready")
            base_done = sem("base_done")
            res_done = sem("res_done")
            stored = [sem(f"stored{i}") for i in range(2)]
            GATE_STEPS = 8

            block = c3.enter_context(nc.Block())

            @block.sync
            def _(sp):
                sp.dma_start(wo_sb[:], w_out.rearrange("(k p) n -> p k n", p=P)).then_inc(wo_in, 16)

                def load(b, c):
                    n = CPB * b + c
                    wait(sp, base_done, TPC * (n - 1))
                    at = bass.ds(S * (b % B) + CH * c, CH)
                    sp.dma_start(xr[:, c % 2], x[at, :].rearrange("(t p) e -> p t e", p=P)).then_inc(rows_in[c % 2], 16)
                    sp.dma_start(yr[:, c % 2], ffn_d[at, :].rearrange("(t p) e -> p t e", p=P)).then_inc(rows_in[c % 2], 16)

                def store(b, c):
                    n = CPB * b + c
                    wait(sp, res_done, TPC * (n + 1))
                    sp.dma_start(out[bass.ds(S * b + CH * c, CH), :].rearrange("(t p) e -> p t e", p=P), res[:, c % 2]) \
                        .then_inc(stored[c % 2], 16)

                load(0, 0)
                load(0, 1)
                def batch(b):
                    for c in range(CPB):
                        if c + 2 < CPB:
                            load(b, c + 2)
                        else:
                            load(b + 1, c + 2 - CPB)
                        store(b, c)

                batch(0)
                with sp.Fori(1, B) as b:
                    batch(b)
                for i in range(2):
                    sp.wait_ge(rows_in[i], 32 * (CPB // 2 * B + 1))
                for i in range(2):
                    sp.wait_ge(stored[i], 16 * CPB // 2 * B)

            @block.scalar
            def _(act):
                act.wait_ge(top_done, TILES + 1)
                nc.scalar.activation(top_x[:], top[:], ACT.Exp).then_inc(top_exp, 1)

                def pack(b, c):
                    n = CPB * b + c
                    wait(act, a_turned, n - 1)
                    for t in range(TPC):
                        last = nc.scalar.activation(rows[:, c % 2, t].rearrange("p (h d) -> p h d", d=D),
                                                    v_all[:, bass.ds(H * b, H), TPC * c + t, :], ACT.Copy)
                    last.then_inc(packed, 1)

                def chunk(b, c):
                    n = CPB * b + c
                    pack(b, c)
                    wait(act, a_turned, n + 1)
                    wait(act, proj_ready, TPC * (n - 1))
                    nc.scalar.activation(turned[:, c % 2, 0], ps[:, 0], ACT.Copy).then_inc(a_copied_a, 1)

                for c in range(CPB):
                    chunk(0, c)
                with act.Fori(1, B) as b:
                    for c in range(CPB):
                        chunk(b, c)

            @block.vector
            def _(dve):
                for t in range(TILES):
                    last = nc.vector.max(top[:, t], logits[:, t])
                    last.then_inc(top_done, 1)
                dve.wait_ge(top_done, TILES)
                nc.vector.tensor_tensor(top_x[:], top[:], top[:, :, 0:1].to_broadcast([P, TILES, NX]), ALU.subtract).then_inc(gate_step, 1)
                dve.wait_ge(gate_step, 1)
                nc.vector.tensor_copy(top[:], top_x[:]).then_inc(top_done, 1)
                dve.wait_ge(top_exp, 1)
                steps = [
                    lambda: nc.vector.tensor_reduce(total[:], top_x[:], AX.X, ALU.add),
                    lambda: nc.vector.reciprocal(total[:], total[:]),
                    lambda: nc.vector.tensor_tensor(share[:], top_x[:, :, 0:2], total[:].unsqueeze(2).to_broadcast([P, TILES, 2]), ALU.mult),
                    lambda: nc.vector.tensor_reduce(total[:], share[:], AX.X, ALU.add),
                    lambda: nc.vector.reciprocal(total[:], total[:]),
                    lambda: nc.vector.tensor_tensor(share[:], share[:], total[:].unsqueeze(2).to_broadcast([P, TILES, 2]), ALU.mult),
                    lambda: nc.vector.tensor_reduce(gate[:], share[:], AX.X, ALU.add),
                ]
                for i, step in enumerate(steps):
                    step().then_inc(gate_step, 1)
                    dve.wait_ge(gate_step, i + 2)

                def chunk(b, c):
                    n = CPB * b + c
                    wait(dve, a_turned, n + 1)
                    wait(dve, proj_ready, TPC * (n - 1))
                    nc.vector.tensor_copy(turned[:, c % 2, 1], ps[:, 1]).then_inc(a_copied_v, 1)
                    wait(dve, rows_in[c % 2], 32 * (CPB // 2 * b + c // 2 + 1))
                    wait(dve, stored[c % 2], 16 * (CPB // 2 * b + c // 2))
                    for t in range(TPC):
                        nc.vector.scalar_tensor_tensor(res[:, c % 2, t], yr[:, c % 2, t], gate[:, bass.ds(KB * b + TPC * c + t, 1)],
                                                       xr[:, c % 2, t], ALU.mult, ALU.add).then_inc(base_done, 1)
                    for t in range(TPC):
                        wait(dve, base_done, TPC * n + t + 1)
                        wait(dve, proj_ready, TPC * n + t + 1)
                        nc.vector.tensor_tensor(res[:, c % 2, t], res[:, c % 2, t], ps[:, 2 + t, 0:E], ALU.add).then_inc(res_done, 1)

                for c in range(CPB):
                    chunk(0, c)
                with dve.Fori(1, B) as b:
                    for c in range(CPB):
                        chunk(b, c)

            @block.tensor
            def _(pe):
                def chunk(b, c):
                    n = CPB * b + c
                    wait(pe, packed, n + 1)
                    wait(pe, a_copied_a, n)
                    wait(pe, a_copied_v, n)
                    for t in range(TPC):
                        for k in range(KE):
                            last = nc.tensor.transpose(ps[:, k, P * t:P * (t + 1)], rows[:, c % 2, t, P * k:P * (k + 1)], ident[:])
                    last.then_inc(a_turned, 1)
                    wait(pe, a_copied_a, n + 1)
                    wait(pe, a_copied_v, n + 1)
                    for t in range(TPC):
                        wait(pe, res_done, TPC * (n - 1) + t + 1)
                        for k in range(KE):
                            last = nc.tensor.matmul(ps[:, 2 + t, 0:E], turned[:, c % 2, k, P * t:P * (t + 1)], wo_sb[:, k],
                                                    start=k == 0, stop=k == KE - 1)
                        last.then_inc(proj_ready, 1)

                pe.wait_ge(wo_in, 16)
                for c in range(CPB):
                    chunk(0, c)
                with pe.Fori(1, B) as b:
                    for c in range(CPB):
                        chunk(b, c)


_INS = ["L0_attn_hidden_states", "L0_attn_W_qkv", "L0_attn_W_out", "L0_attn_rel_emb", "L0_ffn_router_w",
        "L0_ffn_w1", "L0_ffn_b1", "L0_ffn_w2", "L0_ffn_b2"]


def kernel(**inputs):
    import numpy as np
    import concourse.bacc as bacc
    from concourse.bass_utils import run_bass_kernel_spmd

    nc = bacc.Bacc("TRN2", target_bir_lowering=False, num_devices=1)
    arrays, args = {}, []
    for name in _INS + ["bucket_line"]:
        a = bucket_line() if name == "bucket_line" else np.ascontiguousarray(inputs[name])
        if name == _INS[0]:
            a = a.reshape(B * S, E)
        arrays[f"in_{name}"] = a
        args.append(nc.dram_tensor(f"in_{name}", a.shape, mybir.dt.from_np(a.dtype), kind="ExternalInput").ap())
    args.append(nc.dram_tensor("out_rows", (B * S, E), F32, kind="ExternalOutput").ap())
    transformer_layer(nc, *args)
    r = run_bass_kernel_spmd(nc, [arrays], core_ids=[0])
    return r.results[0]["out_rows"].reshape(B, S, E)
```

```python
import concourse.bass as bass
from concourse import mybir
from contextlib import ExitStack

F32 = mybir.dt.float32
F32R = mybir.dt.float32r
BF16 = mybir.dt.bfloat16
ALU = mybir.AluOpType
ACT = mybir.ActivationFunctionType
AX = mybir.AxisListType

B, S, E = 4, 2048, 256
H, D = 16, 16
F = 1024
NX = 8
P = 128
CH = 512
KE = E // P
KF = F // P
TPC = CH // P
CPB = S // CH
KB = S // P
NH = B * H
TILES = B * KB
EPS = 1e-5

BUCKETS = 32
NEAR = 96
NQ = P + 2 * NEAR
LINE = NQ + P

PARTS = 3
PAIRS = 6
ROWS = PAIRS * D
GROUP = 4
GROUPS = NH // GROUP
LEAD = 4


def bucket_line():
    import numpy as np

    half = BUCKETS // 2
    exact = half // 2
    firsts = [next(n for n in range(exact, 200) if n * n >= exact * exact * 2**j) for j in range(half - exact)]
    hot = np.zeros((BUCKETS, LINE), np.float32)
    for x in range(LINE):
        rel = P + NEAR - 1 - x
        n = abs(rel)
        bucket = n if n < exact else exact - 1 + sum(n >= f for f in firsts)
        hot[bucket + (half if rel > 0 else 0), x] = 1.0
    return hot


def wait(eng, sem, value):
    if not isinstance(value, int) or value > 0:
        eng.wait_ge(sem, value)


def transformer_layer(nc, x, w_qkv, w_out, rel_emb, router_w, w1, b1, w2, b2, hot, out):
    qk_d = nc.dram_tensor("qk_parts", [2, PARTS, NH * D, S], BF16).ap()
    line_d = nc.dram_tensor("bias_line", [H, LINE], F32).ap()
    near_d = nc.dram_tensor("bias_near", [NH, P, NQ], F32).ap()
    ffn_d = nc.dram_tensor("ffn_rows", [B * S, E], F32).ap()

    ctx = ExitStack()
    with ctx:
        def sb(name, shape, dt=F32, c=ctx):
            return c.enter_context(nc.sbuf_tensor(name, shape, dt))

        def sem(name):
            return ctx.enter_context(nc.semaphore(name))

        ps = ctx.enter_context(nc.psum_tensor("ps", [P, 8, CH], F32))
        ident = sb("ident", [P, P])
        v_all = sb("v_all", [P, NH, KB, D])
        logits = sb("logits", [P, TILES, NX])

        c1 = ExitStack()
        with c1:
            W_SIZES = [2 * KE * E, KE * (E + NX), KE * F, KF * E]
            W_QK, W_VR, W_1, W_2 = range(4)
            w_parts = [sb(f"w_parts{i}", [P, 2, n], F32R, c=c1) for i, n in enumerate(W_SIZES)]
            w_raw = [v_all[:].rearrange("p n k d -> p (n k d)")[:, NH * KB * D - sum(W_SIZES[i:]):][:, 0:n]
                     for i, n in enumerate(W_SIZES)]

            def weight(i, part, k):
                blocks = KF if i == W_2 else KE
                return w_parts[i][:, part].rearrange("p (k n) -> p k n", k=blocks)[:, k]

            RAWS = 3
            PASSES = [(0, 0), (0, 1), (1, 0)]
            b1_sb = sb("b1_sb", [P, KF], c=c1)
            b2_sb = sb("b2_sb", [P, E], c=c1)
            emb_sb = sb("emb_sb", [BUCKETS, H], c=c1)
            hot_sb = sb("hot_sb", [BUCKETS, LINE], c=c1)
            line_sb = sb("line_sb", [H, LINE], c=c1)
            line_exp = sb("line_exp", [H, LINE], c=c1)
            power = sb("power", [P, TPC], c=c1)
            x_sb = sb("x_sb", [P, 2, TPC, E], c=c1)
            stats = sb("stats", [P, TPC, 6], c=c1)
            mean_var = sb("mean_var", [P, TPC, 2], c=c1)
            var_eps = sb("var_eps", [P, TPC], c=c1)
            rstd = sb("rstd", [P, TPC], c=c1)
            xn = sb("xn", [P, TPC, E], c=c1)
            xnt = sb("xnt", [P, 2, KE, CH], F32R, c=c1)
            parts = sb("parts", [P, 2 * KE, PARTS, CH], BF16, c=c1)
            rest = sb("rest", [P, 2 * KE, CH], c=c1)
            hid_raw = sb("hid_raw", [P, RAWS, CH], c=c1)
            hid = sb("hid", [P, 2, KF, CH], F32R, c=c1)
            ffn_sb = sb("ffn_sb", [P, 2, TPC, E], c=c1)

            w_loaded = sem("w_loaded")
            line_in = sem("line_in")
            ident_zeroed = sem("ident_zeroed")
            ident_made = sem("ident_made")
            line_mm = sem("line_mm")
            line_shifted = sem("line_shifted")
            line_ready = sem("line_ready")
            line_stored = sem("line_stored")
            near_stored = sem("near_stored")
            x_loaded = [sem(f"x_loaded{i}") for i in range(2)]
            stats_done = sem("stats_done")
            aggr_done = sem("aggr_done")
            var_done = sem("var_done")
            rstd_done = sem("rstd_done")
            xn_done = sem("xn_done")
            xt_ready = sem("xt_ready")
            xt_high = sem("xt_high")
            xt_low = sem("xt_low")
            w_high = [sem(f"w_high{i}") for i in range(4)]
            w_low = [sem(f"w_low{i}") for i in range(4)]
            w_in = [sem(f"w_in{i}") for i in range(4)]
            hid_high = sem("hid_high")
            hid_low = sem("hid_low")
            qk_ready = sem("qk_ready")
            hi_done = sem("hi_done")
            rest_done = sem("rest_done")
            mid_done = sem("mid_done")
            lo_done = sem("lo_done")
            parts_stored = [sem(f"parts_stored{i}") for i in range(2 * KE)]
            vr_ready = sem("vr_ready")
            v_copied = sem("v_copied")
            r_copied = sem("r_copied")
            f1_ready = sem("f1_ready")
            gelu_done = sem("gelu_done")
            f2_ready = sem("f2_ready")
            f2_copied = sem("f2_copied")
            ffn_stored = [sem(f"ffn_stored{i}") for i in range(2)]
            W_LOADS = 2
            BANKS = [2, 3, 6, 7]

            block = c1.enter_context(nc.Block())

            @block.sync
            def _(sp):
                sp.dma_start(emb_sb[:], rel_emb).then_inc(line_in, 16)
                sp.dma_start(hot_sb[:], hot).then_inc(line_in, 16)

                def load_x(b, c):
                    wait(sp, xn_done, CPB * b + c - 1)
                    sp.dma_start(x_sb[:, c % 2], x[bass.ds(S * (b % B) + CH * c, CH), :].rearrange("(t p) e -> p t e", p=P)) \
                        .then_inc(x_loaded[c % 2], 16)

                load_x(0, 0)
                load_x(0, 1)
                def raw(i, n):
                    return w_raw[i].rearrange("p (k n) -> p k n", n=n)

                sp.dma_start(raw(W_QK, 2 * E), w_qkv[:, 0:2 * E].rearrange("(k p) n -> p k n", p=P)).then_inc(w_in[W_QK], 16)
                sp.dma_start(raw(W_VR, E + NX)[:, :, 0:E], w_qkv[:, 2 * E:3 * E].rearrange("(k p) n -> p k n", p=P)).then_inc(w_in[W_VR], 16)
                sp.dma_start(raw(W_VR, E + NX)[:, :, E:E + NX], router_w.rearrange("(k p) n -> p k n", p=P)).then_inc(w_in[W_VR], 16)
                sp.dma_start(raw(W_1, F), w1.rearrange("(k p) n -> p k n", p=P)).then_inc(w_in[W_1], 16)
                sp.dma_start(raw(W_2, E), w2.rearrange("(k p) n -> p k n", p=P)).then_inc(w_in[W_2], 16)
                sp.dma_start(b1_sb[:], b1.rearrange("(k p) -> p k", p=P), allow_slow_non_contiguous=True).then_inc(w_loaded, 16)
                sp.dma_start(b2_sb[:], bass.AP(tensor=b2.tensor, offset=0, ap=[[0, P], [1, E]])).then_inc(w_loaded, 16)

                sp.wait_ge(line_ready, 1)
                sp.dma_start(line_d, line_exp[:]).then_inc(line_stored, 16)
                sp.wait_ge(line_stored, 16)
                for b in range(B):
                    sp.dma_start(near_d[H * b:H * (b + 1)],
                                 bass.AP(tensor=line_d.tensor, offset=P - 1, ap=[[LINE, H], [-1, P], [1, NQ]])) \
                        .then_inc(near_stored, 16)

                def chunk(b, c):
                    for m in range(2 * KE):
                        wait(sp, lo_done, 2 * KE * (CPB * b + c) + m + 1)
                        sp.dma_start(qk_d[m // KE, :, bass.ds(E * b + P * (m % KE), P), CH * c:CH * (c + 1)].rearrange("s r n -> r s n"),
                                     parts[:, m]).then_inc(parts_stored[m], 16)
                    wait(sp, f2_copied, TPC * (CPB * b + c + 1))
                    sp.dma_start(ffn_d[bass.ds(S * b + CH * c, CH), :].rearrange("(t p) e -> p t e", p=P), ffn_sb[:, c % 2]) \
                        .then_inc(ffn_stored[c % 2], 16)

                def batch(b):
                    for c in range(CPB):
                        if c + 2 < CPB:
                            load_x(b, c + 2)
                        else:
                            load_x(b + 1, c + 2 - CPB)
                        chunk(b, c)

                batch(0)
                with sp.Fori(1, B) as b:
                    batch(b)
                sp.wait_ge(x_loaded[0], 16 * (CPB // 2 * B + 1))
                sp.wait_ge(x_loaded[1], 16 * (CPB // 2 * B + 1))
                sp.wait_ge(near_stored, 16 * B)
                for m in range(2 * KE):
                    sp.wait_ge(parts_stored[m], 16 * CPB * B)
                for i in range(2):
                    sp.wait_ge(ffn_stored[i], 16 * CPB // 2 * B)

            @block.gpsimd
            def _(pool):
                nc.gpsimd.memset(ident[:], 0.0).then_inc(ident_zeroed, 1)
                pool.wait_ge(ident_zeroed, 1)
                nc.gpsimd.affine_select(out=ident[:], in_=ident[:], compare_op=ALU.not_equal, fill=1.0, base=0,
                                        pattern=[[-1, P]], channel_multiplier=1).then_inc(ident_made, 1)
                nc.gpsimd.memset(power[:], -0.5).then_inc(ident_made, 1)
                pool.wait_ge(ident_made, 2)

                def norm(n):
                    wait(pool, var_done, n + 1)
                    wait(pool, xn_done, n)
                    nc.gpsimd.tensor_tensor(rstd[:], var_eps[:], power[:], ALU.pow).then_inc(rstd_done, 1)

                def chunk(n):
                    for m in range(2 * KE):
                        i = 2 * KE * n + m
                        wait(pool, mid_done, i + 1)
                        nc.gpsimd.tensor_tensor(parts[:, m, 2], rest[:, m], parts[:, m, 1], ALU.subtract) \
                            .then_inc(lo_done, 1)

                def batch(b):
                    for c in range(CPB):
                        norm(CPB * b + c + 1)
                        chunk(CPB * b + c)

                norm(0)
                batch(0)
                with pool.Fori(1, B) as b:
                    batch(b)

            @block.vector
            def _(dve):
                dve.wait_ge(line_mm, 1)
                nc.vector.tensor_scalar(line_sb[:], ps[0:H, 7, 0:LINE], ps[0:H, 7, LINE - 1:LINE], None, ALU.subtract) \
                    .then_inc(line_shifted, 1)

                def norm_stats(b, c):
                    n = CPB * b + c
                    wait(dve, x_loaded[c % 2], 16 * (CPB // 2 * b + c // 2 + 1))
                    for t in range(TPC):
                        last = nc.vector.bn_stats(stats[:, t], x_sb[:, c % 2, t])
                    last.then_inc(stats_done, 1)
                    wait(dve, stats_done, n + 1)

                def norm_var(n):
                    for t in range(TPC):
                        last = nc.vector.bn_aggr(mean_var[:, t], stats[:, t])
                    last.then_inc(aggr_done, 1)
                    wait(dve, aggr_done, n + 1)
                    nc.vector.tensor_scalar(var_eps[:], mean_var[:, :, 1], EPS, None, ALU.add).then_inc(var_done, 1)

                def scale(b, c):
                    n = CPB * b + c
                    wait(dve, rstd_done, n + 1)
                    wait(dve, xt_ready, n)
                    for t in range(TPC):
                        last = nc.vector.tensor_scalar(xn[:, t], x_sb[:, c % 2, t], mean_var[:, t, 0:1], rstd[:, t:t + 1],
                                                       ALU.subtract, ALU.mult)
                    last.then_inc(xn_done, 1)

                def low(n):
                    for k in range(KE):
                        wait(dve, xt_high, KE * n + k + 1)
                        nc.vector.tensor_tensor(xnt[:, 1, k], ps[:, k], xnt[:, 0, k].bitcast(F32), ALU.subtract).then_inc(xt_low, 1)

                def w_low_part(i):
                    dve.wait_ge(w_high[i], 1)
                    nc.vector.tensor_tensor(w_parts[i][:, 1], w_raw[i], w_parts[i][:, 0].bitcast(F32), ALU.subtract).then_inc(w_low[i], 1)

                def chunk(b, c):
                    n = CPB * b + c
                    nb, ncc = (b, c + 1) if c + 1 < CPB else (b + 1, 0)
                    norm_stats(nb, ncc)
                    for m in range(2 * KE):
                        i = 2 * KE * n + m
                        if m == 1:
                            norm_var(n + 1)
                        wait(dve, hi_done, i + 1)
                        wait(dve, lo_done, i + 1 - 2 * KE)
                        nc.vector.tensor_tensor(rest[:, m], ps[:, BANKS[m]], parts[:, m, 0], ALU.subtract) \
                            .then_inc(rest_done, 1)
                    for f in range(KF):
                        if f == KF // 2:
                            scale(nb, ncc)
                        wait(dve, hid_high, KF * n + f + 1)
                        if f == 0:
                            wait(dve, f2_ready, TPC * n)
                        nc.vector.tensor_tensor(hid[:, 1, f], hid_raw[:, f % RAWS], hid[:, 0, f].bitcast(F32), ALU.subtract).then_inc(hid_low, 1)
                        if isinstance(n, int) and n == 0 and f == 0:
                            w_low_part(W_2)
                    low(n + 1)
                    for t in range(TPC):
                        wait(dve, f2_ready, TPC * n + t + 1)
                        if t == 0:
                            wait(dve, ffn_stored[c % 2], 16 * (CPB // 2 * b + c // 2))
                        nc.vector.tensor_tensor(ffn_sb[:, c % 2, t], ps[:, 6 + t % 2, E * (t // 2):E * (t // 2 + 1)], b2_sb[:],
                                                ALU.add).then_inc(f2_copied, 1)

                dve.wait_ge(w_loaded, 16 * W_LOADS)
                norm_stats(0, 0)
                norm_var(0)
                scale(0, 0)
                w_low_part(W_QK)
                low(0)
                w_low_part(W_1)
                w_low_part(W_VR)
                for c in range(CPB):
                    chunk(0, c)
                with dve.Fori(1, B) as b:
                    for c in range(CPB):
                        chunk(b, c)

            @block.scalar
            def _(act):
                act.wait_ge(line_shifted, 1)
                nc.scalar.activation(line_exp[:], line_sb[:], ACT.Exp).then_inc(line_ready, 1)

                def high(n):
                    for k in range(KE):
                        wait(act, xt_ready, n + 1)
                        wait(act, vr_ready, TPC * n)
                        nc.scalar.activation(xnt[:, 0, k], ps[:, k], ACT.Copy).then_inc(xt_high, 1)

                def w_high_part(i):
                    act.wait_ge(w_in[i], 32 if i == W_VR else 16)
                    nc.scalar.activation(w_parts[i][:, 0], w_raw[i], ACT.Copy).then_inc(w_high[i], 1)

                def chunk(b, c):
                    n = CPB * b + c
                    for m in range(2 * KE + 1):
                        i = 2 * KE * n + m
                        if m < 2 * KE:
                            wait(act, qk_ready, i + 1)
                            wait(act, parts_stored[m], 16 * n)
                            nc.scalar.activation(parts[:, m, 0], ps[:, BANKS[m]], ACT.Copy).then_inc(hi_done, 1)
                        if m > 0:
                            wait(act, rest_done, i)
                            nc.scalar.activation(parts[:, m - 1, 1], rest[:, m - 1], ACT.Copy).then_inc(mid_done, 1)
                    for f in range(KF + 1):
                        if f < KF:
                            wait(act, f1_ready, KF * n + f + 1)
                            wait(act, hid_low, KF * n + f + 1 - RAWS if f >= RAWS else KF * n)
                            if isinstance(n, int) and n == 0 and f == 0:
                                act.wait_ge(w_loaded, 16 * W_LOADS)
                            nc.scalar.activation(hid_raw[:, f % RAWS], ps[:, 4 + f % 2], ACT.Gelu_apprx_tanh, bias=b1_sb[:, f:f + 1]) \
                                .then_inc(gelu_done, 1)
                        if f > 0:
                            wait(act, gelu_done, KF * n + f)
                            if f == 1:
                                wait(act, f2_ready, TPC * n)
                            nc.scalar.activation(hid[:, 0, f - 1], hid_raw[:, (f - 1) % RAWS], ACT.Copy).then_inc(hid_high, 1)
                    for t in range(TPC):
                        wait(act, vr_ready, TPC * n + t + 1)
                        nc.scalar.activation(v_all[:, bass.ds(H * b, H), TPC * c + t, :],
                                             ps[:, BANKS[t], 0:E].rearrange("p (h d) -> p h d", d=D), ACT.Copy) \
                            .then_inc(v_copied, 1)
                        nc.scalar.activation(logits[:, bass.ds(KB * b + TPC * c + t, 1), :].rearrange("p a n -> p (a n)"),
                                             ps[:, BANKS[t], E:E + NX], ACT.Copy).then_inc(r_copied, 1)
                    high(n + 1)

                w_high_part(W_QK)
                high(0)
                for i in (W_1, W_VR, W_2):
                    w_high_part(i)
                for c in range(CPB):
                    chunk(0, c)
                with act.Fori(1, B) as b:
                    for c in range(CPB):
                        chunk(b, c)

            @block.tensor
            def _(pe):
                pe.wait_ge(line_in, 32)
                nc.tensor.matmul(ps[0:H, 7, 0:LINE], emb_sb[:], hot_sb[:], start=True, stop=True).then_inc(line_mm, 1)
                pe.wait_ge(ident_made, 2)
                pe.wait_ge(line_shifted, 1)

                def transposes(n):
                    wait(pe, xn_done, n + 1)
                    wait(pe, xt_low, KE * n)
                    for t in range(TPC):
                        for k in range(KE):
                            last = nc.tensor.transpose(ps[:, k, P * t:P * (t + 1)], xn[:, t, P * k:P * (k + 1)], ident[:])
                    last.then_inc(xt_ready, 1)

                def product(to, stationary, moving, blocks):
                    for k in range(blocks):
                        for a, b in PASSES:
                            last = nc.tensor.matmul(to, stationary(a, k), moving(b, k), start=k == 0 and (a, b) == PASSES[0],
                                                    stop=k == blocks - 1 and (a, b) == PASSES[-1])
                    return last

                def chunk(b, c):
                    n = CPB * b + c
                    first = isinstance(n, int) and n == 0
                    wait(pe, xt_low, KE * (n + 1))
                    for m in range(2 * KE):
                        if m < 2:
                            wait(pe, r_copied, TPC * (n - 1) + m + 1)
                        else:
                            wait(pe, f2_copied, TPC * (n - 1) + m + 1)
                        if first and m == 0:
                            pe.wait_ge(w_low[W_QK], 1)
                        product(ps[:, BANKS[m]], lambda a, k: weight(W_QK, a, k)[:, P * m:P * (m + 1)], lambda a, k: xnt[:, a, k], KE) \
                            .then_inc(qk_ready, 1)
                    for f in range(KF):
                        wait(pe, gelu_done, KF * n + f - 1)
                        if first and f == 0:
                            pe.wait_ge(w_low[W_1], 1)
                        product(ps[:, 4 + f % 2], lambda a, k: weight(W_1, a, k)[:, P * f:P * (f + 1)], lambda a, k: xnt[:, a, k], KE) \
                            .then_inc(f1_ready, 1)
                    for t in range(TPC):
                        wait(pe, rest_done, 2 * KE * n + t + 1)
                        if first and t == 0:
                            pe.wait_ge(w_low[W_VR], 1)
                        product(ps[:, BANKS[t], 0:E + NX], lambda a, k: xnt[:, a, k, P * t:P * (t + 1)], lambda a, k: weight(W_VR, a, k), KE) \
                            .then_inc(vr_ready, 1)
                    transposes(n + 1)
                    if first:
                        pe.wait_ge(w_low[W_2], 1)
                    for t in range(TPC):
                        if t < 2:
                            wait(pe, r_copied, TPC * n + 3 + t)
                        else:
                            wait(pe, f2_copied, TPC * n + t - 1)
                        for f in range(KF):
                            if t == 0:
                                wait(pe, hid_low, KF * n + f + 1)
                            for a, b_ in PASSES:
                                last = nc.tensor.matmul(ps[:, 6 + t % 2, E * (t // 2):E * (t // 2 + 1)], hid[:, a, f, P * t:P * (t + 1)],
                                                        weight(W_2, b_, f), start=f == 0 and (a, b_) == PASSES[0],
                                                        stop=f == KF - 1 and (a, b_) == PASSES[-1])
                        last.then_inc(f2_ready, 1)

                transposes(0)
                for c in range(CPB):
                    chunk(0, c)
                with pe.Fori(1, B) as b:
                    for c in range(CPB):
                        chunk(b, c)

        c2 = ExitStack()
        with c2:
            q_st = [sb(f"q_st{u}", [ROWS + 1, S], BF16, c=c2) for u in range(GROUP)]
            k_st = [sb(f"k_st{u}", [ROWS + 1, S], BF16, c=c2) for u in range(GROUP)]
            near = [sb(f"near{u}", [P, NQ], c=c2) for u in range(GROUP)]
            vx = sb("vx", [P, 2, KB, 32], c=c2)
            vr = sb("vr", [P, 2, KB, 32], c=c2)
            prob = sb("prob", [P, 2, S], c=c2)
            max_half = sb("max_half", [P, 2, KB, 2], c=c2)
            max_neg = sb("max_neg", [P, 2, KB], c=c2)
            shift_row = sb("shift_row", [KB, 2, P], BF16, c=c2)
            o_sb = sb("o_sb", [P, CH], c=c2)
            o_turned_sb = sb("o_turned_sb", [P, TPC, CPB, 32], c=c2)
            recip = sb("recip", [P, TPC, CPB], c=c2)

            stacks_in = [sem(f"stacks_in{u}") for u in range(GROUP)]
            shift_in = [sem(f"shift_in{u}") for u in range(GROUP)]
            near_in = [sem(f"near_in{u}") for u in range(GROUP)]
            ones_set = sem("ones_set")
            score_ready = sem("score_ready")
            drained = sem("drained")
            near_done = sem("near_done")
            pv_done = sem("pv_done")
            v_read = sem("v_read")
            v_built = sem("v_built")
            max_ready = sem("max_ready")
            max_done = sem("max_done")
            neg_done = sem("neg_done")
            shift_turned = sem("shift_turned")
            o_copied = sem("o_copied")
            o_turned = sem("o_turned")
            recip_done = sem("recip_done")
            o_done = sem("o_done")

            STACK_LOADS = 2 * PAIRS
            Q_PART = [0, 0, 0, 1, 1, 2]
            K_PART = [0, 1, 2, 0, 1, 0]

            def near_span(kb):
                first = P * kb - NEAR
                return max(first, 0), min(first + NQ, S), max(-first, 0)

            RING = 3
            MAX_BANK = RING
            SUM_BANK = 7
            TURN_RESULT, TURN_SHIFT = 3, 13
            RESULT_AT = CPB * TURN_RESULT
            SHIFT_AT = CPB * TURN_SHIFT + 1
            RING_TILES = CPB * KB + 2

            def tile_at(kb, c):
                return CPB * kb + c + (kb >= TURN_RESULT) + (kb >= TURN_SHIFT)

            def drained_at(n, at):
                count = RING_TILES * n + at + 1
                if isinstance(n, int):
                    count += (n == 0 and at < RESULT_AT) - (n == NH - 1 and at >= SHIFT_AT)
                return count

            def max_at(n, step):
                return (n + 1, step + LEAD) if step + LEAD < KB else (n + 2, step + LEAD - KB)

            block = c2.enter_context(nc.Block())

            @block.sync
            def _(sp):
                def load(n, u):
                    wait(sp, score_ready, CPB * KB * (n - GROUP + 1))
                    for i in range(PAIRS):
                        sp.dma_start(q_st[u][D * i:D * (i + 1), :], qk_d[0, Q_PART[i], bass.ds(D * n, D), :]).then_inc(stacks_in[u], 16)
                        sp.dma_start(k_st[u][D * i:D * (i + 1), :], qk_d[1, K_PART[i], bass.ds(D * n, D), :]).then_inc(stacks_in[u], 16)
                    wait(sp, near_done, KB * (n - GROUP + 1))
                    sp.dma_start(near[u][:], near_d[bass.ds(n, 1)].rearrange("a p c -> (a p) c")).then_inc(near_in[u], 16)

                def shift(n, u):
                    wait(sp, drained, 1 if isinstance(n, int) and n == 0 else drained_at(n - 1, SHIFT_AT))
                    sp.dma_start(q_st[u][ROWS:ROWS + 1, :].rearrange("a (i p) -> a i p", p=P), shift_row[:, n % 2 if isinstance(n, int) else u % 2, :]) \
                        .then_inc(shift_in[u], 16)

                def group(g, last=False):
                    for u in range(GROUP):
                        n = GROUP * g + u
                        if not (last and u > 0):
                            load(n + 3, (u + 3) % GROUP)
                        if not (last and u == GROUP - 1):
                            shift(n + 1, (u + 1) % GROUP)

                for u in range(3):
                    load(u, u)
                shift(0, 0)
                group(0)
                with sp.Fori(1, GROUPS - 1) as g:
                    group(g)
                group(GROUPS - 1, last=True)

            @block.scalar
            def _(act):
                def shift(n, par):
                    wait(act, shift_turned, n + 1)
                    nc.scalar.activation(shift_row[:, par % 2, :], ps[0:KB, SHIFT_AT % RING, 0:P], ACT.Copy).then_inc(drained, 1)

                def collect(n):
                    wait(act, pv_done, CPB * KB * (n + 1))
                    wait(act, o_turned, n)
                    nc.scalar.activation(o_sb[:], ps[:, SUM_BANK], ACT.Copy).then_inc(o_copied, 1)

                def collect_turned(n):
                    wait(act, o_turned, n + 1)
                    wait(act, o_done, n)
                    nc.scalar.activation(o_turned_sb[:].rearrange("p i c w -> p (i c w)"), ps[:, RESULT_AT % RING], ACT.Copy) \
                        .then_inc(drained, 1)

                def head(n, u, first=False, last=False):
                    for kb in range(KB):
                        if kb == 1 and not first:
                            collect(n - 1)
                        if kb == TURN_RESULT and not first:
                            collect_turned(n - 1)
                        if kb == TURN_SHIFT and not last:
                            shift(n + 1, (u + 1) % GROUP)
                        for c in range(CPB):
                            i = CPB * (KB * n + kb) + c
                            wait(act, score_ready, i + 1)
                            wait(act, pv_done, i - 2 * CPB + 1)
                            nc.scalar.activation(prob[:, kb % 2, CH * c:CH * (c + 1)], ps[:, tile_at(kb, c) % RING], ACT.Exp).then_inc(drained, 1)

                shift(0, 0)
                for u in range(GROUP):
                    head(u, u, first=u == 0)
                with act.Fori(1, GROUPS - 1) as g:
                    for u in range(GROUP):
                        head(GROUP * g + u, u)
                for u in range(GROUP):
                    head(NH - GROUP + u, u, last=u == GROUP - 1)
                collect(NH - 1)
                collect_turned(NH - 1)

            @block.gpsimd
            def _(pool):
                def build(n, u, turn):
                    wait(pool, pv_done, CPB * KB * (n - 1))
                    pool.wait_ge(ones_set, GROUP + 2)
                    nc.gpsimd.tensor_copy(vx[:, u % 2, :, 0:D], v_all[:, bass.ds(n, 1)].rearrange("p a k d -> p (a k) d")) \
                        .then_inc(v_read, 1)
                    pool.wait_ge(near_in[u], 16 * turn)
                    wait(pool, v_read, n + 1)
                    nc.gpsimd.tensor_tensor(vr[:, u % 2], vx[:, u % 2],
                                            near[u][:, 0:1].unsqueeze(2).to_broadcast([P, KB, 32]), ALU.mult).then_inc(v_built, 1)

                def normalise(n):
                    nc.gpsimd.tensor_tensor(
                        v_all[:, bass.ds(n, 1)].rearrange("p a (c i) d -> p i (a c) d", c=CPB), o_turned_sb[:, :, :, 0:D],
                        recip[:].unsqueeze(3).to_broadcast([P, TPC, CPB, D]), ALU.mult).then_inc(o_done, 1)

                def head(g, u, first=False, last=False):
                    n = GROUP * g + u
                    for kb in range(KB):
                        if kb == TURN_RESULT + 2 and not first:
                            wait(pool, recip_done, n)
                            wait(pool, v_read, n)
                        if kb == 8 and not last:
                            build(n + 1, (u + 1) % GROUP, g + 1 if u + 1 < GROUP else g + 2)
                        q0, q1, c0 = near_span(kb)
                        wait(pool, drained, drained_at(n, tile_at(kb, (q1 - 1) // CH)))
                        nc.gpsimd.tensor_tensor(prob[:, kb % 2, q0:q1], prob[:, kb % 2, q0:q1], near[u][:, c0:c0 + q1 - q0],
                                                ALU.mult).then_inc(near_done, 1)
                        if kb == TURN_RESULT + 2 and not first:
                            normalise(n - 1)

                build(0, 0, 1)
                for u in range(GROUP):
                    head(0, u, first=u == 0)
                with pool.Fori(1, GROUPS - 1) as g:
                    for u in range(GROUP):
                        head(g, u)
                for u in range(GROUP):
                    head(GROUPS - 1, u, last=u == GROUP - 1)
                wait(pool, recip_done, NH)
                wait(pool, v_read, NH)
                normalise(NH - 1)

            @block.vector
            def _(dve):
                def maxima(m, par, i):
                    for half in range(2):
                        wait(dve, max_ready, 2 * (KB * m + i) + half + 1)
                        if i == 0 and half == 0:
                            wait(dve, neg_done, m - 1)
                        nc.vector.reduce_max(max_half[:, par % 2, i, half:half + 1],
                                             ps[:, MAX_BANK + 2 * half:MAX_BANK + 2 + 2 * half].rearrange("p a n -> p (a n)"), AX.X).then_inc(max_done, 1)

                def combine(m, par):
                    wait(dve, max_done, 2 * KB * (m + 1))
                    wait(dve, shift_turned, m - 1)
                    nc.vector.tensor_reduce(max_neg[:, par % 2], max_half[:, par % 2], AX.X, ALU.max, negate=True).then_inc(neg_done, 1)

                def reciprocals(n, copied):
                    wait(dve, drained, copied)
                    wait(dve, o_done, n)
                    nc.vector.reciprocal(recip[:], o_turned_sb[:, :, :, D]).then_inc(recip_done, 1)

                def head(n, u, first=False, left=2):
                    for kb in range(KB):
                        ahead = 1 if kb + LEAD < KB else 2
                        m, i = max_at(n, kb)
                        if ahead <= left:
                            maxima(m, (u + ahead) % 2, i)
                        if kb == TURN_RESULT and not first:
                            reciprocals(n - 1, drained_at(n, RESULT_AT))
                        if kb == KB - 1 - LEAD and left >= 1:
                            combine(n + 1, u + 1)

                for u in range(GROUP):
                    nc.vector.memset(k_st[u][ROWS:ROWS + 1, :], 1.0).then_inc(ones_set, 1)
                nc.vector.memset(vx[:, :, :, D + 1:32], 0.0).then_inc(ones_set, 1)
                nc.vector.memset(vx[:, :, :, D:D + 1], 1.0).then_inc(ones_set, 1)
                for i in range(KB):
                    maxima(0, 0, i)
                combine(0, 0)
                for i in range(LEAD):
                    maxima(1, 1, i)
                for u in range(GROUP):
                    head(u, u, first=u == 0)
                with dve.Fori(1, GROUPS - 1) as g:
                    for u in range(GROUP):
                        head(GROUP * g + u, u)
                for u in range(GROUP):
                    head(NH - GROUP + u, u, left=GROUP - 1 - u)
                reciprocals(NH - 1, drained_at(NH - 1, RING_TILES - 1) + 1)

            @block.tensor
            def _(pe):
                pe.wait_ge(ones_set, GROUP + 2)

                def maxima(m, u, i, c):
                    if c % 2 == 0:
                        wait(pe, max_done, 2 * (KB * m + i) + c // 2 - 1)
                    mm = nc.tensor.matmul(ps[:, MAX_BANK + c], q_st[u][0:ROWS, P * i:P * (i + 1)], k_st[u][0:ROWS, CH * c:CH * (c + 1)],
                                          start=True, stop=True)
                    if c % 2 == 1:
                        mm.then_inc(max_ready, 1)

                def ring_free(n, at):
                    wait(pe, drained, drained_at(n, at - RING))

                def turn_shift(m, par):
                    wait(pe, neg_done, m + 1)
                    nc.tensor.transpose(ps[0:KB, SHIFT_AT % RING, 0:P], max_neg[:, par % 2], ident[:]).then_inc(shift_turned, 1)

                def scores(n, u, kb, c):
                    ring_free(n, tile_at(kb, c))
                    nc.tensor.matmul(ps[:, tile_at(kb, c) % RING], k_st[u][:, P * kb:P * (kb + 1)], q_st[u][:, CH * c:CH * (c + 1)],
                                     start=True, stop=True).then_inc(score_ready, 1)

                def values(n, u, kb, c):
                    q0, q1, _ = near_span(kb)
                    lo, hi = CH * c, CH * (c + 1)
                    if q0 < hi and q1 > lo:
                        wait(pe, near_done, KB * n + kb + 1)
                    else:
                        wait(pe, drained, drained_at(n, tile_at(kb, c)))
                    if kb == 0 and c == 0:
                        wait(pe, v_built, n + 1)
                        wait(pe, o_copied, n)
                    cut = min(max(P * kb - NEAR, lo), hi)
                    for v, a, z in ((vr, lo, cut), (vx, cut, hi)):
                        if a < z:
                            last = nc.tensor.matmul(ps[32 * c:32 * (c + 1), SUM_BANK, a - lo:z - lo], v[:, u % 2, kb],
                                                    prob[:, kb % 2, a:z], start=kb == 0, stop=kb == KB - 1 and z == hi)
                    last.then_inc(pv_done, 1)

                def turn_result(n):
                    wait(pe, o_copied, n + 1)
                    for i in range(TPC):
                        last = nc.tensor.transpose(ps[:, RESULT_AT % RING, P * i:P * (i + 1)], o_sb[:, P * i:P * (i + 1)], ident[:])
                    last.then_inc(o_turned, 1)

                def sums(n, u, kb, first):
                    for c in range(CPB):
                        if kb > 0:
                            values(n, u, kb - 1, c)
                        elif not first:
                            values(n - 1, u + 1, KB - 1, c)

                def head(g, u, first=False, left=2):
                    n = GROUP * g + u
                    for kb in range(KB):
                        ahead = 1 if kb + LEAD < KB else 2
                        m, i = max_at(n, kb)
                        mu = (u + ahead) % GROUP
                        if kb == 0:
                            pe.wait_ge(shift_in[u], 16 * (g + 1))
                        if i == 0 and ahead <= left:
                            pe.wait_ge(stacks_in[mu], 16 * STACK_LOADS * (g + 1 + (u + ahead) // GROUP))
                        if kb == TURN_RESULT and not first:
                            ring_free(n, RESULT_AT)
                            turn_result(n - 1)
                        if kb == TURN_SHIFT and left >= 1:
                            ring_free(n, SHIFT_AT)
                            turn_shift(n + 1, u + 1)
                        for c in range(CPB):
                            scores(n, u, kb, c)
                            if c == CPB // 2:
                                sums(n, u, kb, first)
                            if ahead <= left:
                                maxima(m, mu, i, c)

                for m in range(2):
                    pe.wait_ge(stacks_in[m], 16 * STACK_LOADS)
                    for i in range(KB if m == 0 else LEAD):
                        for c in range(CPB):
                            maxima(m, m, i, c)
                    if m == 0:
                        turn_shift(0, 0)
                for u in range(GROUP):
                    head(0, u, first=u == 0)
                with pe.Fori(1, GROUPS - 1) as g:
                    for u in range(GROUP):
                        head(g, u)
                for u in range(GROUP):
                    head(GROUPS - 1, u, left=GROUP - 1 - u)
                for c in range(CPB):
                    values(NH - 1, NH - 1, KB - 1, c)
                ring_free(NH - 1, RING_TILES - 1 + RING)
                turn_result(NH - 1)

        c3 = ExitStack()
        with c3:
            wo_sb = sb("wo_sb", [P, KE, E], c=c3)
            top = sb("top", [P, TILES, NX], c=c3)
            top_x = sb("top_x", [P, TILES, NX], c=c3)
            total = sb("total", [P, TILES], c=c3)
            share = sb("share", [P, TILES, 2], c=c3)
            gate = sb("gate", [P, TILES], c=c3)
            xr = sb("xr", [P, 2, TPC, E], c=c3)
            yr = sb("yr", [P, 2, TPC, E], c=c3)
            res = sb("res", [P, 2, TPC, E], c=c3)
            rows = sb("rows", [P, 2, TPC, E], c=c3)
            turned = sb("turned", [P, 2, KE, CH], c=c3)

            wo_in = sem("wo_in")
            top_done = sem("top_done")
            top_exp = sem("top_exp")
            gate_step = sem("gate_step")
            rows_in = [sem(f"rows_in{i}") for i in range(2)]
            packed = sem("packed")
            a_turned = sem("a_turned")
            a_copied_a = sem("a_copied_a")
            a_copied_v = sem("a_copied_v")
            proj_ready = sem("proj_ready")
            base_done = sem("base_done")
            res_done = sem("res_done")
            stored = [sem(f"stored{i}") for i in range(2)]
            GATE_STEPS = 8

            block = c3.enter_context(nc.Block())

            @block.sync
            def _(sp):
                sp.dma_start(wo_sb[:], w_out.rearrange("(k p) n -> p k n", p=P)).then_inc(wo_in, 16)

                def load(b, c):
                    n = CPB * b + c
                    wait(sp, base_done, TPC * (n - 1))
                    at = bass.ds(S * (b % B) + CH * c, CH)
                    sp.dma_start(xr[:, c % 2], x[at, :].rearrange("(t p) e -> p t e", p=P)).then_inc(rows_in[c % 2], 16)
                    sp.dma_start(yr[:, c % 2], ffn_d[at, :].rearrange("(t p) e -> p t e", p=P)).then_inc(rows_in[c % 2], 16)

                def store(b, c):
                    n = CPB * b + c
                    wait(sp, res_done, TPC * (n + 1))
                    sp.dma_start(out[bass.ds(S * b + CH * c, CH), :].rearrange("(t p) e -> p t e", p=P), res[:, c % 2]) \
                        .then_inc(stored[c % 2], 16)

                load(0, 0)
                load(0, 1)
                def batch(b):
                    for c in range(CPB):
                        if c + 2 < CPB:
                            load(b, c + 2)
                        else:
                            load(b + 1, c + 2 - CPB)
                        store(b, c)

                batch(0)
                with sp.Fori(1, B) as b:
                    batch(b)
                for i in range(2):
                    sp.wait_ge(rows_in[i], 32 * (CPB // 2 * B + 1))
                for i in range(2):
                    sp.wait_ge(stored[i], 16 * CPB // 2 * B)

            @block.scalar
            def _(act):
                act.wait_ge(top_done, TILES + 1)
                nc.scalar.activation(top_x[:], top[:], ACT.Exp).then_inc(top_exp, 1)

                def pack(b, c):
                    n = CPB * b + c
                    wait(act, a_turned, n - 1)
                    for t in range(TPC):
                        last = nc.scalar.activation(rows[:, c % 2, t].rearrange("p (h d) -> p h d", d=D),
                                                    v_all[:, bass.ds(H * b, H), TPC * c + t, :], ACT.Copy)
                    last.then_inc(packed, 1)

                def chunk(b, c):
                    n = CPB * b + c
                    pack(b, c)
                    wait(act, a_turned, n + 1)
                    wait(act, proj_ready, TPC * (n - 1))
                    nc.scalar.activation(turned[:, c % 2, 0], ps[:, 0], ACT.Copy).then_inc(a_copied_a, 1)

                for c in range(CPB):
                    chunk(0, c)
                with act.Fori(1, B) as b:
                    for c in range(CPB):
                        chunk(b, c)

            @block.vector
            def _(dve):
                for t in range(TILES):
                    last = nc.vector.max(top[:, t], logits[:, t])
                    last.then_inc(top_done, 1)
                dve.wait_ge(top_done, TILES)
                nc.vector.tensor_tensor(top_x[:], top[:], top[:, :, 0:1].to_broadcast([P, TILES, NX]), ALU.subtract).then_inc(gate_step, 1)
                dve.wait_ge(gate_step, 1)
                nc.vector.tensor_copy(top[:], top_x[:]).then_inc(top_done, 1)
                dve.wait_ge(top_exp, 1)
                steps = [
                    lambda: nc.vector.tensor_reduce(total[:], top_x[:], AX.X, ALU.add),
                    lambda: nc.vector.reciprocal(total[:], total[:]),
                    lambda: nc.vector.tensor_tensor(share[:], top_x[:, :, 0:2], total[:].unsqueeze(2).to_broadcast([P, TILES, 2]), ALU.mult),
                    lambda: nc.vector.tensor_reduce(total[:], share[:], AX.X, ALU.add),
                    lambda: nc.vector.reciprocal(total[:], total[:]),
                    lambda: nc.vector.tensor_tensor(share[:], share[:], total[:].unsqueeze(2).to_broadcast([P, TILES, 2]), ALU.mult),
                    lambda: nc.vector.tensor_reduce(gate[:], share[:], AX.X, ALU.add),
                ]
                for i, step in enumerate(steps):
                    step().then_inc(gate_step, 1)
                    dve.wait_ge(gate_step, i + 2)

                def chunk(b, c):
                    n = CPB * b + c
                    wait(dve, a_turned, n + 1)
                    wait(dve, proj_ready, TPC * (n - 1))
                    nc.vector.tensor_copy(turned[:, c % 2, 1], ps[:, 1]).then_inc(a_copied_v, 1)
                    wait(dve, rows_in[c % 2], 32 * (CPB // 2 * b + c // 2 + 1))
                    wait(dve, stored[c % 2], 16 * (CPB // 2 * b + c // 2))
                    for t in range(TPC):
                        nc.vector.scalar_tensor_tensor(res[:, c % 2, t], yr[:, c % 2, t], gate[:, bass.ds(KB * b + TPC * c + t, 1)],
                                                       xr[:, c % 2, t], ALU.mult, ALU.add).then_inc(base_done, 1)
                    for t in range(TPC):
                        wait(dve, base_done, TPC * n + t + 1)
                        wait(dve, proj_ready, TPC * n + t + 1)
                        nc.vector.tensor_tensor(res[:, c % 2, t], res[:, c % 2, t], ps[:, 2 + t, 0:E], ALU.add).then_inc(res_done, 1)

                for c in range(CPB):
                    chunk(0, c)
                with dve.Fori(1, B) as b:
                    for c in range(CPB):
                        chunk(b, c)

            @block.tensor
            def _(pe):
                def chunk(b, c):
                    n = CPB * b + c
                    wait(pe, packed, n + 1)
                    wait(pe, a_copied_a, n)
                    wait(pe, a_copied_v, n)
                    for t in range(TPC):
                        for k in range(KE):
                            last = nc.tensor.transpose(ps[:, k, P * t:P * (t + 1)], rows[:, c % 2, t, P * k:P * (k + 1)], ident[:])
                    last.then_inc(a_turned, 1)
                    wait(pe, a_copied_a, n + 1)
                    wait(pe, a_copied_v, n + 1)
                    for t in range(TPC):
                        wait(pe, res_done, TPC * (n - 1) + t + 1)
                        for k in range(KE):
                            last = nc.tensor.matmul(ps[:, 2 + t, 0:E], turned[:, c % 2, k, P * t:P * (t + 1)], wo_sb[:, k],
                                                    start=k == 0, stop=k == KE - 1)
                        last.then_inc(proj_ready, 1)

                pe.wait_ge(wo_in, 16)
                for c in range(CPB):
                    chunk(0, c)
                with pe.Fori(1, B) as b:
                    for c in range(CPB):
                        chunk(b, c)


_INS = ["L0_attn_hidden_states", "L0_attn_W_qkv", "L0_attn_W_out", "L0_attn_rel_emb", "L0_ffn_router_w",
        "L0_ffn_w1", "L0_ffn_b1", "L0_ffn_w2", "L0_ffn_b2"]


def kernel(**inputs):
    import numpy as np
    import concourse.bacc as bacc
    from concourse.bass_utils import run_bass_kernel_spmd

    nc = bacc.Bacc("TRN2", target_bir_lowering=False, num_devices=1)
    arrays, args = {}, []
    for name in _INS + ["bucket_line"]:
        a = bucket_line() if name == "bucket_line" else np.ascontiguousarray(inputs[name])
        if name == _INS[0]:
            a = a.reshape(B * S, E)
        arrays[f"in_{name}"] = a
        args.append(nc.dram_tensor(f"in_{name}", a.shape, mybir.dt.from_np(a.dtype), kind="ExternalInput").ap())
    args.append(nc.dram_tensor("out_rows", (B * S, E), F32, kind="ExternalOutput").ap())
    transformer_layer(nc, *args)
    r = run_bass_kernel_spmd(nc, [arrays], core_ids=[0])
    return r.results[0]["out_rows"].reshape(B, S, E)
```

```python
import concourse.bass as bass
from concourse import mybir
from contextlib import ExitStack
import math

F32 = mybir.dt.float32
F32R = mybir.dt.float32r
BF16 = mybir.dt.bfloat16
ALU = mybir.AluOpType
ACT = mybir.ActivationFunctionType
AX = mybir.AxisListType

B, S, E = 4, 2048, 256
H, D = 16, 16
F = 1024
NX = 8
P = 128
CH = 512
KE = E // P
KF = F // P
TPC = CH // P
CPB = S // CH
KB = S // P
NH = B * H
EPS = 1e-5

BUCKETS = 32
NEAR = 96
NQ = P + 2 * NEAR
LINE = NQ + P

PARTS = 3
PAIRS = 6
ROWS = PAIRS * D
GROUP = 4
GROUPS = NH // GROUP
LEAD = 4

PASSES = [(0, 0), (0, 1), (1, 0)]

Q_LOADS = [(0, 0, 1, 3), (3, 1, 1, 2), (5, 2, 1, 1)]
K_LOADS = [(0, 0, 3, 1), (3, 0, 2, 1), (5, 0, 1, 1)]
STACK_LOADS = len(Q_LOADS) + len(K_LOADS)

EARLY_QK = {1: 0, 3: 1}
EARLY_BATCHES = B - 2
EARLY_IN_BATCH = 2 * (KB + LEAD) // EARLY_BATCHES


def early_pieces(b, c):
    own = KB // (EARLY_BATCHES * CPB)
    pieces = [(1, CPB // 2 * (b - 1) + c // 2, half) for half in range(2)] if c % 2 == 0 else []
    return pieces + [(0, own * (CPB * (b - 1) + c) + i, half) for i in range(own) for half in range(2)]


def early_at(c, t):
    return t + (len(EARLY_QK) if c % 2 == 0 else 0)


def early_count(b, c):
    return EARLY_IN_BATCH * (b - 1) + sum(len(early_pieces(1, i)) for i in range(c))


def bucket_line():
    import numpy as np

    half = BUCKETS // 2
    exact = half // 2
    firsts = [next(n for n in range(exact, 200) if n * n >= exact * exact * 2**j) for j in range(half - exact)]
    hot = np.zeros((BUCKETS, LINE), np.float32)
    for x in range(LINE):
        rel = P + NEAR - 1 - x
        n = abs(rel)
        bucket = n if n < exact else exact - 1 + sum(n >= f for f in firsts)
        hot[bucket + (half if rel > 0 else 0), x] = 1.0
    return hot


def wait(eng, sem, value):
    if not isinstance(value, int) or value > 0:
        eng.wait_ge(sem, value)


def transformer_layer(nc, x, w_qkv, w_out, rel_emb, router_w, w1, b1, w2, b2, hot, out):
    qk_d = nc.dram_tensor("qk_parts", [2, PARTS, NH * D, S], BF16).ap()
    line_d = nc.dram_tensor("bias_line", [H, LINE], F32).ap()
    near_d = nc.dram_tensor("bias_near", [H, P, NQ], F32).ap()
    base_d = nc.dram_tensor("base_rows", [B * S, E], F32).ap()

    def load_stacks(sp, n, q_stack, k_stack, loaded):
        for which, stack, loads in ((0, q_stack, Q_LOADS), (1, k_stack, K_LOADS)):
            for row, part, parts, copies in loads:
                rows = qk_d[which, part:part + parts, bass.ds(D * n, D), :]
                if copies > 1:
                    rows = rows.to_broadcast([copies, D, S])
                sp.dma_start(stack[D * row:D * (row + parts * copies), :], rows).then_inc(loaded, 16)

    ctx = ExitStack()
    with ctx:
        def sb(name, shape, dt=F32, c=ctx):
            return c.enter_context(nc.sbuf_tensor(name, shape, dt))

        def sem(name):
            return ctx.enter_context(nc.semaphore(name))

        ps = ctx.enter_context(nc.psum_tensor("ps", [P, 8, CH], F32))
        ident = sb("ident", [P, P])
        v_all = sb("v_all", [P, NH, KB, D])
        max_half = sb("max_half", [P, 2, KB, 2])
        max_ready = sem("max_ready")
        max_done = sem("max_done")

        c1 = ExitStack()
        with c1:
            W_SIZES = [2 * KE * E, KE * (E + NX), KE * F, KF * E]
            W_QK, W_VR, W_1, W_2 = range(4)
            w_parts = [sb(f"w_parts{i}", [P, 2, n], F32R, c=c1) for i, n in enumerate(W_SIZES)]
            w_raw = [v_all[:].rearrange("p n k d -> p (n k d)")[:, NH * KB * D - sum(W_SIZES[i:]):][:, 0:n]
                     for i, n in enumerate(W_SIZES)]

            early = v_all[:, NH - H:NH].rearrange("p n k d -> p (n k d)").bitcast(BF16).rearrange("p (a n) -> p a n", n=S)
            q_early, k_early = ([early[:, 2 * h + i] for h in range(2)] for i in range(2))

            def weight(i, part, k):
                blocks = KF if i == W_2 else KE
                return w_parts[i][:, part].rearrange("p (k n) -> p k n", k=blocks)[:, k]

            RAWS = 3
            b1_sb = sb("b1_sb", [P, KF], c=c1)
            b2_sb = sb("b2_sb", [P, E], c=c1)
            emb_sb = sb("emb_sb", [BUCKETS, H], c=c1)
            hot_sb = sb("hot_sb", [BUCKETS, LINE], c=c1)
            line_sb = sb("line_sb", [H, LINE], c=c1)
            line_exp = sb("line_exp", [H, LINE], c=c1)
            power = sb("power", [P, TPC], c=c1)
            x_sb = sb("x_sb", [P, CPB, TPC, E], c=c1)
            stats = sb("stats", [P, TPC, 6], c=c1)
            mean_var = sb("mean_var", [P, TPC, 2], c=c1)
            var_eps = sb("var_eps", [P, TPC], c=c1)
            rstd = sb("rstd", [P, TPC], c=c1)
            xn = sb("xn", [P, TPC, E], c=c1)
            xnt = sb("xnt", [P, 2, KE, CH], F32R, c=c1)
            parts = sb("parts", [P, 2 * KE, PARTS, CH], BF16, c=c1)
            rest = sb("rest", [P, 2 * KE, CH], c=c1)
            hid_raw = sb("hid_raw", [P, RAWS, CH], c=c1)
            hid = sb("hid", [P, 2, KF, CH], F32R, c=c1)
            ffn_sb = sb("ffn_sb", [P, TPC, E], c=c1)
            logits = sb("logits", [P, TPC, NX], c=c1)
            top = sb("top", [P, TPC, NX], c=c1)
            top_less = sb("top_less", [P, TPC, NX], c=c1)
            top_exp = sb("top_exp", [P, TPC, NX], c=c1)
            euler = sb("euler", [P, TPC, NX], c=c1)
            total = sb("total", [P, TPC], c=c1)
            share = sb("share", [P, TPC, 2], c=c1)
            gate = sb("gate", [P, TPC], c=c1)

            w_loaded = sem("w_loaded")
            line_in = sem("line_in")
            ident_zeroed = sem("ident_zeroed")
            ident_made = sem("ident_made")
            line_mm = sem("line_mm")
            line_shifted = sem("line_shifted")
            line_ready = sem("line_ready")
            line_stored = sem("line_stored")
            near_stored = sem("near_stored")
            x_loaded = [sem(f"x_loaded{i}") for i in range(CPB)]
            stats_done = sem("stats_done")
            aggr_done = sem("aggr_done")
            var_done = sem("var_done")
            rstd_done = sem("rstd_done")
            xn_done = sem("xn_done")
            xt_ready = sem("xt_ready")
            xt_high = sem("xt_high")
            xt_low = sem("xt_low")
            w_high = [sem(f"w_high{i}") for i in range(4)]
            w_low = [sem(f"w_low{i}") for i in range(4)]
            w_in = [sem(f"w_in{i}") for i in range(4)]
            hid_high = sem("hid_high")
            hid_low = sem("hid_low")
            qk_ready = sem("qk_ready")
            hi_done = sem("hi_done")
            rest_done = sem("rest_done")
            mid_done = sem("mid_done")
            lo_done = sem("lo_done")
            parts_stored = [sem(f"parts_stored{i}") for i in range(2 * KE)]
            vr_ready = sem("vr_ready")
            r_copied = sem("r_copied")
            f1_ready = sem("f1_ready")
            gelu_done = sem("gelu_done")
            f2_ready = sem("f2_ready")
            f2_copied = sem("f2_copied")
            base_done = sem("base_done")
            base_stored = [sem(f"base_stored{i}") for i in range(CPB)]
            top_done = sem("top_done")
            less_done = sem("less_done")
            exp_done = sem("exp_done")
            gate_step = sem("gate_step")
            early_in = sem("early_in")
            W_LOADS = 2
            GATE_STEPS = 7
            QK_BANKS = [2, 3, 6, 7]
            F1_BANKS = [4, 5, 2, 3]
            VR_BANKS = [6, 7, 2, 3]
            F2_BANKS = [6, 7]

            block = c1.enter_context(nc.Block())

            @block.sync
            def _(sp):
                def load_x(b, c):
                    wait(sp, base_stored[c], 16 * b)
                    sp.dma_start(x_sb[:, c], x[bass.ds(S * (b % B) + CH * c, CH), :].rearrange("(t p) e -> p t e", p=P)) \
                        .then_inc(x_loaded[c], 16)

                def store_base(b, c):
                    wait(sp, base_done, TPC * (CPB * b + c + 1))
                    sp.dma_start(base_d[bass.ds(S * b + CH * c, CH), :].rearrange("(t p) e -> p t e", p=P), x_sb[:, c]) \
                        .then_inc(base_stored[c], 16)

                def raw(i, n):
                    return w_raw[i].rearrange("p (k n) -> p k n", n=n)

                load_x(0, 0)
                sp.dma_start(emb_sb[:], rel_emb).then_inc(line_in, 16)
                sp.dma_start(hot_sb[:], hot).then_inc(line_in, 16)
                sp.dma_start(raw(W_QK, 2 * E), w_qkv[:, 0:2 * E].rearrange("(k p) n -> p k n", p=P)).then_inc(w_in[W_QK], 16)
                sp.dma_start(raw(W_1, F), w1.rearrange("(k p) n -> p k n", p=P)).then_inc(w_in[W_1], 16)
                sp.dma_start(raw(W_VR, E + NX)[:, :, 0:E], w_qkv[:, 2 * E:3 * E].rearrange("(k p) n -> p k n", p=P)).then_inc(w_in[W_VR], 16)
                sp.dma_start(raw(W_VR, E + NX)[:, :, E:E + NX], router_w.rearrange("(k p) n -> p k n", p=P)).then_inc(w_in[W_VR], 16)
                load_x(0, 1)
                sp.dma_start(b1_sb[:], b1.rearrange("(k p) -> p k", p=P), allow_slow_non_contiguous=True).then_inc(w_loaded, 16)
                sp.dma_start(b2_sb[:], bass.AP(tensor=b2.tensor, offset=0, ap=[[0, P], [1, E]])).then_inc(w_loaded, 16)
                sp.dma_start(raw(W_2, E), w2.rearrange("(k p) n -> p k n", p=P)).then_inc(w_in[W_2], 16)

                sp.wait_ge(line_ready, 1)
                sp.dma_start(line_d, line_exp[:]).then_inc(line_stored, 16)
                sp.wait_ge(line_stored, 16)
                sp.dma_start(near_d, bass.AP(tensor=line_d.tensor, offset=P - 1, ap=[[LINE, H], [-1, P], [1, NQ]])) \
                    .then_inc(near_stored, 16)

                def chunk(b, c):
                    for m in range(2 * KE):
                        wait(sp, lo_done, 2 * KE * (CPB * b + c) + m + 1)
                        sp.dma_start(qk_d[m // KE, :, bass.ds(E * b + P * (m % KE), P), CH * c:CH * (c + 1)].rearrange("s r n -> r s n"),
                                     parts[:, m]).then_inc(parts_stored[m], 16)
                    load_x(b + (c + 2) // CPB, (c + 2) % CPB)
                    if c > 0:
                        store_base(b, c - 1)
                    elif not (isinstance(b, int) and b == 0):
                        store_base(b - 1, CPB - 1)

                def batch(b):
                    for c in range(CPB):
                        chunk(b, c)

                batch(0)
                for i in range(4):
                    sp.wait_ge(w_low[i], 1)
                for m in range(2 * KE):
                    sp.wait_ge(parts_stored[m], 16 * CPB)
                for h in range(2):
                    load_stacks(sp, h, q_early[h], k_early[h], early_in)
                with sp.Fori(1, B) as b:
                    batch(b)
                store_base(B - 1, CPB - 1)
                for c in range(CPB):
                    sp.wait_ge(x_loaded[c], 16 * (B + (c < 2)))
                sp.wait_ge(near_stored, 16)
                for m in range(2 * KE):
                    sp.wait_ge(parts_stored[m], 16 * CPB * B)
                for c in range(CPB):
                    sp.wait_ge(base_stored[c], 16 * B)

            @block.gpsimd
            def _(pool):
                nc.gpsimd.memset(ident[:], 0.0).then_inc(ident_zeroed, 1)
                pool.wait_ge(ident_zeroed, 1)
                nc.gpsimd.affine_select(out=ident[:], in_=ident[:], compare_op=ALU.not_equal, fill=1.0, base=0,
                                        pattern=[[-1, P]], channel_multiplier=1).then_inc(ident_made, 1)
                nc.gpsimd.memset(power[:], -0.5).then_inc(ident_made, 1)
                nc.gpsimd.memset(euler[:], math.e).then_inc(ident_made, 1)
                pool.wait_ge(ident_made, 3)

                def norm(n):
                    wait(pool, var_done, n + 1)
                    wait(pool, xn_done, n)
                    nc.gpsimd.tensor_tensor(rstd[:], var_eps[:], power[:], ALU.pow).then_inc(rstd_done, 1)

                def chunk(n):
                    for m in range(2 * KE):
                        i = 2 * KE * n + m
                        wait(pool, mid_done, i + 1)
                        nc.gpsimd.tensor_tensor(parts[:, m, 2], rest[:, m], parts[:, m, 1], ALU.subtract) \
                            .then_inc(lo_done, 1)

                def exps(n):
                    wait(pool, less_done, n + 1)
                    wait(pool, gate_step, GATE_STEPS * n)
                    nc.gpsimd.tensor_tensor(top_exp[:], euler[:], top_less[:], ALU.pow).then_inc(exp_done, 1)

                def batch(b):
                    for c in range(CPB):
                        chunk(CPB * b + c)
                        norm(CPB * b + c + 1)
                        exps(CPB * b + c)

                norm(0)
                batch(0)
                with pool.Fori(1, B) as b:
                    batch(b)

            @block.vector
            def _(dve):
                def norm_stats(b, c):
                    n = CPB * b + c
                    wait(dve, x_loaded[c], 16 * (b + 1))
                    for t in range(TPC):
                        last = nc.vector.bn_stats(stats[:, t], x_sb[:, c, t])
                    last.then_inc(stats_done, 1)
                    wait(dve, stats_done, n + 1)

                def norm_var(n):
                    for t in range(TPC):
                        last = nc.vector.bn_aggr(mean_var[:, t], stats[:, t])
                    last.then_inc(aggr_done, 1)
                    wait(dve, aggr_done, n + 1)
                    nc.vector.tensor_scalar(var_eps[:], mean_var[:, :, 1], EPS, None, ALU.add).then_inc(var_done, 1)

                def scale(b, c):
                    n = CPB * b + c
                    wait(dve, rstd_done, n + 1)
                    wait(dve, xt_ready, n)
                    for t in range(TPC):
                        last = nc.vector.tensor_scalar(xn[:, t], x_sb[:, c, t], mean_var[:, t, 0:1], rstd[:, t:t + 1],
                                                       ALU.subtract, ALU.mult)
                    last.then_inc(xn_done, 1)

                def low(n):
                    for k in range(KE):
                        wait(dve, xt_high, KE * n + k + 1)
                        nc.vector.tensor_tensor(xnt[:, 1, k], ps[:, k], xnt[:, 0, k].bitcast(F32), ALU.subtract).then_inc(xt_low, 1)

                def sort(n):
                    for t in range(TPC):
                        last = nc.vector.max(top[:, t], logits[:, t])
                    last.then_inc(top_done, 1)
                    wait(dve, top_done, n + 1)
                    wait(dve, exp_done, n)
                    nc.vector.tensor_tensor(top_less[:], top[:], top[:, :, 0:1].to_broadcast([P, TPC, NX]), ALU.subtract) \
                        .then_inc(less_done, 1)

                def scales(n):
                    wait(dve, exp_done, n + 1)
                    steps = [
                        lambda: nc.vector.tensor_reduce(total[:], top_exp[:], AX.X, ALU.add),
                        lambda: nc.vector.reciprocal(total[:], total[:]),
                        lambda: nc.vector.tensor_tensor(share[:], top_exp[:, :, 0:2], total[:].unsqueeze(2).to_broadcast([P, TPC, 2]), ALU.mult),
                        lambda: nc.vector.tensor_reduce(total[:], share[:], AX.X, ALU.add),
                        lambda: nc.vector.reciprocal(total[:], total[:]),
                        lambda: nc.vector.tensor_tensor(share[:], share[:], total[:].unsqueeze(2).to_broadcast([P, TPC, 2]), ALU.mult),
                        lambda: nc.vector.tensor_reduce(gate[:], share[:], AX.X, ALU.add),
                    ]
                    for i, step in enumerate(steps):
                        step().then_inc(gate_step, 1)
                        wait(dve, gate_step, GATE_STEPS * n + i + 1)

                def add_base(n, c, t):
                    nc.vector.scalar_tensor_tensor(x_sb[:, c, t], ffn_sb[:, t], gate[:, t:t + 1], x_sb[:, c, t], ALU.mult, ALU.add) \
                        .then_inc(base_done, 1)

                def w_low_part(i):
                    dve.wait_ge(w_high[i], 1)
                    nc.vector.tensor_tensor(w_parts[i][:, 1], w_raw[i], w_parts[i][:, 0].bitcast(F32), ALU.subtract).then_inc(w_low[i], 1)

                def early_max(b, c, piece):
                    h, i, half = early_pieces(b, c)[piece]
                    nc.vector.reduce_max(max_half[:, h, bass.ds(i, 1), half], ps[:, 0:2].rearrange("p a n -> p (a n)"), AX.X).then_inc(max_done, 1)

                def chunk(b, c, early=False, last=False):
                    n = CPB * b + c
                    nb, ncc = (b, c + 1) if c + 1 < CPB else (b + 1, 0)
                    first = isinstance(n, int) and n == 0
                    for m in range(2 * KE):
                        i = 2 * KE * n + m
                        piece = EARLY_QK.get(m) if early and c % 2 == 0 else None
                        if piece is not None:
                            wait(dve, max_ready, early_count(b, c) + piece + 1)
                        wait(dve, hi_done, i + 1)
                        wait(dve, lo_done, i + 1 - 2 * KE)
                        nc.vector.tensor_tensor(rest[:, m], ps[:, QK_BANKS[m]], parts[:, m, 0], ALU.subtract) \
                            .then_inc(rest_done, 1)
                        if piece is not None:
                            early_max(b, c, piece)
                    if not first:
                        scales(n - 1)
                        wait(dve, f2_copied, TPC * n)
                    norm_stats(nb, ncc)
                    for f in range(KF):
                        if f == 1:
                            norm_var(n + 1)
                        if f == KF // 2:
                            scale(nb, ncc)
                        wait(dve, hid_high, KF * n + f + 1)
                        if f == 0:
                            wait(dve, f2_ready, TPC * n)
                        nc.vector.tensor_tensor(hid[:, 1, f], hid_raw[:, f % RAWS], hid[:, 0, f].bitcast(F32), ALU.subtract).then_inc(hid_low, 1)
                        if f < TPC and not first:
                            add_base(n - 1, (c - 1) % CPB, f)
                        if first and f == 0:
                            w_low_part(W_2)
                    wait(dve, r_copied, TPC * (n + 1))
                    low(n + 1)
                    sort(n)
                    if first:
                        dve.wait_ge(w_loaded, 16 * W_LOADS)
                    for t in range(TPC):
                        wait(dve, f2_ready, TPC * n + t + 1)
                        wait(dve, base_done, TPC * (n - 1) + t + 1)
                        if early:
                            wait(dve, max_ready, early_count(b, c) + early_at(c, t) + 1)
                        nc.vector.tensor_tensor(ffn_sb[:, t], ps[:, F2_BANKS[t % 2], E * (t // 2):E * (t // 2 + 1)], b2_sb[:],
                                                ALU.add).then_inc(f2_copied, 1)
                        if early:
                            early_max(b, c, early_at(c, t))
                        if last and t >= TPC - 2:
                            if t == TPC - 2:
                                scales(n)
                            wait(dve, f2_copied, TPC * n + t + 1)
                            for i in range(0 if t == TPC - 2 else t, t + 1):
                                add_base(n, c, i)

                norm_stats(0, 0)
                norm_var(0)
                dve.wait_ge(line_mm, 1)
                nc.vector.tensor_scalar(line_sb[:], ps[0:H, 7, 0:LINE], ps[0:H, 7, LINE - 1:LINE], None, ALU.subtract) \
                    .then_inc(line_shifted, 1)
                scale(0, 0)
                w_low_part(W_QK)
                low(0)
                w_low_part(W_1)
                w_low_part(W_VR)
                for c in range(CPB):
                    chunk(0, c)
                with dve.Fori(1, B - 1) as b:
                    for c in range(CPB):
                        chunk(b, c, early=True)
                for c in range(CPB):
                    chunk(B - 1, c, last=c == CPB - 1)

            @block.scalar
            def _(act):
                act.wait_ge(line_shifted, 1)
                nc.scalar.activation(line_exp[:], line_sb[:], ACT.Exp).then_inc(line_ready, 1)

                def high(n):
                    for k in range(KE):
                        wait(act, xt_ready, n + 1)
                        wait(act, vr_ready, TPC * n)
                        nc.scalar.activation(xnt[:, 0, k], ps[:, k], ACT.Copy).then_inc(xt_high, 1)

                def w_high_part(i):
                    act.wait_ge(w_in[i], 32 if i == W_VR else 16)
                    nc.scalar.activation(w_parts[i][:, 0], w_raw[i], ACT.Copy).then_inc(w_high[i], 1)

                def chunk(b, c):
                    n = CPB * b + c
                    for m in range(2 * KE + 1):
                        i = 2 * KE * n + m
                        if m < 2 * KE:
                            wait(act, qk_ready, i + 1)
                            wait(act, parts_stored[m], 16 * n)
                            nc.scalar.activation(parts[:, m, 0], ps[:, QK_BANKS[m]], ACT.Copy).then_inc(hi_done, 1)
                        if m > 0:
                            wait(act, rest_done, i)
                            nc.scalar.activation(parts[:, m - 1, 1], rest[:, m - 1], ACT.Copy).then_inc(mid_done, 1)
                    for f in range(KF + 1):
                        if f < KF:
                            wait(act, f1_ready, KF * n + f + 1)
                            wait(act, hid_low, KF * n + f + 1 - RAWS if f >= RAWS else KF * n)
                            if isinstance(n, int) and n == 0 and f == 0:
                                act.wait_ge(w_loaded, 16 * W_LOADS)
                            nc.scalar.activation(hid_raw[:, f % RAWS], ps[:, F1_BANKS[f % 4]], ACT.Gelu_apprx_tanh, bias=b1_sb[:, f:f + 1]) \
                                .then_inc(gelu_done, 1)
                        if f > 0:
                            wait(act, gelu_done, KF * n + f)
                            if f == 1:
                                wait(act, f2_ready, TPC * n)
                            nc.scalar.activation(hid[:, 0, f - 1], hid_raw[:, (f - 1) % RAWS], ACT.Copy).then_inc(hid_high, 1)
                    for t in range(TPC):
                        wait(act, vr_ready, TPC * n + t + 1)
                        nc.scalar.activation(v_all[:, bass.ds(H * b, H), TPC * c + t, :],
                                             ps[:, VR_BANKS[t], 0:E].rearrange("p (h d) -> p h d", d=D), ACT.Copy)
                        wait(act, top_done, n)
                        nc.scalar.activation(logits[:, t], ps[:, VR_BANKS[t], E:E + NX], ACT.Copy).then_inc(r_copied, 1)
                    high(n + 1)

                w_high_part(W_QK)
                high(0)
                for i in (W_1, W_VR, W_2):
                    w_high_part(i)
                for c in range(CPB):
                    chunk(0, c)
                with act.Fori(1, B - 1) as b:
                    for c in range(CPB):
                        chunk(b, c)
                act.wait_ge(max_done, early_count(B - 1, 0))
                for c in range(CPB):
                    chunk(B - 1, c)

            @block.tensor
            def _(pe):
                pe.wait_ge(line_in, 32)
                nc.tensor.matmul(ps[0:H, 7, 0:LINE], emb_sb[:], hot_sb[:], start=True, stop=True).then_inc(line_mm, 1)
                pe.wait_ge(ident_made, 3)
                pe.wait_ge(line_shifted, 1)

                def transposes(n):
                    wait(pe, xn_done, n + 1)
                    wait(pe, xt_low, KE * n)
                    for t in range(TPC):
                        for k in range(KE):
                            last = nc.tensor.transpose(ps[:, k, P * t:P * (t + 1)], xn[:, t, P * k:P * (k + 1)], ident[:])
                    last.then_inc(xt_ready, 1)

                def product(to, stationary, moving, blocks):
                    for k in range(blocks):
                        for a, b in PASSES:
                            last = nc.tensor.matmul(to, stationary(a, k), moving(b, k), start=k == 0 and (a, b) == PASSES[0],
                                                    stop=k == blocks - 1 and (a, b) == PASSES[-1])
                    return last

                def early_scores(b, c, piece):
                    h, i, half = early_pieces(b, c)[piece]
                    wait(pe, max_done, early_count(b, c) + piece)
                    for j in range(2):
                        last = nc.tensor.matmul(ps[:, j], q_early[h][0:ROWS, bass.ds(P * i, P)],
                                                k_early[h][0:ROWS, CH * (2 * half + j):CH * (2 * half + j + 1)], start=True, stop=True)
                    last.then_inc(max_ready, 1)

                def chunk(b, c, early=False):
                    n = CPB * b + c
                    first = isinstance(n, int) and n == 0
                    wait(pe, xt_low, KE * (n + 1))
                    for m in range(2 * KE):
                        if m < 2:
                            wait(pe, r_copied, TPC * (n - 1) + 3 + m)
                        else:
                            wait(pe, f2_copied, TPC * (n - 1) + m + 1)
                        if first and m == 0:
                            pe.wait_ge(w_low[W_QK], 1)
                        product(ps[:, QK_BANKS[m]], lambda a, k: weight(W_QK, a, k)[:, P * m:P * (m + 1)], lambda a, k: xnt[:, a, k], KE) \
                            .then_inc(qk_ready, 1)
                        if early and c % 2 == 0 and m in EARLY_QK:
                            early_scores(b, c, EARLY_QK[m])
                    for f in range(KF):
                        if f in (2, 3):
                            wait(pe, rest_done, 2 * KE * n + f - 1)
                        else:
                            wait(pe, gelu_done, KF * n + max(f - 3, 0))
                        if first and f == 0:
                            pe.wait_ge(w_low[W_1], 1)
                        product(ps[:, F1_BANKS[f % 4]], lambda a, k: weight(W_1, a, k)[:, P * f:P * (f + 1)], lambda a, k: xnt[:, a, k], KE) \
                            .then_inc(f1_ready, 1)
                    for t in range(TPC):
                        if t < 2:
                            wait(pe, rest_done, 2 * KE * n + 3 + t)
                        else:
                            wait(pe, gelu_done, KF * n + KF - 3 + t)
                        if first and t == 0:
                            pe.wait_ge(w_low[W_VR], 1)
                        product(ps[:, VR_BANKS[t], 0:E + NX], lambda a, k: xnt[:, a, k, P * t:P * (t + 1)], lambda a, k: weight(W_VR, a, k), KE) \
                            .then_inc(vr_ready, 1)
                    if early:
                        wait(pe, max_done, early_count(b, c) + early_at(c, 0))
                    transposes(n + 1)
                    if first:
                        pe.wait_ge(w_low[W_2], 1)
                    for t in range(TPC):
                        if t < 2:
                            wait(pe, r_copied, TPC * n + t + 1)
                        else:
                            wait(pe, f2_copied, TPC * n + t - 1)
                        for f in range(KF):
                            if t == 0:
                                wait(pe, hid_low, KF * n + f + 1)
                            for a, b_ in PASSES:
                                last = nc.tensor.matmul(ps[:, F2_BANKS[t % 2], E * (t // 2):E * (t // 2 + 1)], hid[:, a, f, P * t:P * (t + 1)],
                                                        weight(W_2, b_, f), start=f == 0 and (a, b_) == PASSES[0],
                                                        stop=f == KF - 1 and (a, b_) == PASSES[-1])
                        last.then_inc(f2_ready, 1)
                        if early:
                            if t == 0:
                                wait(pe, xt_low, KE * (n + 2))
                            early_scores(b, c, early_at(c, t))

                transposes(0)
                for c in range(CPB):
                    chunk(0, c)
                pe.wait_ge(early_in, 2 * 16 * STACK_LOADS)
                with pe.Fori(1, B - 1) as b:
                    for c in range(CPB):
                        chunk(b, c, early=True)
                pe.wait_ge(max_done, early_count(B - 1, 0))
                for c in range(CPB):
                    chunk(B - 1, c)

        c2 = ExitStack()
        with c2:
            q_st = [sb(f"q_st{u}", [ROWS + 1, S], BF16, c=c2) for u in range(GROUP)]
            k_st = [sb(f"k_st{u}", [ROWS + 1, S], BF16, c=c2) for u in range(GROUP)]
            near = [sb(f"near{u}", [P, NQ], c=c2) for u in range(GROUP)]
            vx = sb("vx", [P, 2, KB, 32], c=c2)
            vr = sb("vr", [P, 2, KB, 32], c=c2)
            prob = sb("prob", [P, 2, S], c=c2)
            max_neg = sb("max_neg", [P, 2, KB], c=c2)
            shift_row = sb("shift_row", [KB, 2, P], BF16, c=c2)
            o_sb = sb("o_sb", [P, CH], c=c2)
            o_turned_sb = sb("o_turned_sb", [P, TPC, CPB, 32], c=c2)
            recip = sb("recip", [P, TPC, CPB], c=c2)

            stacks_in = [sem(f"stacks_in{u}") for u in range(GROUP)]
            shift_in = [sem(f"shift_in{u}") for u in range(GROUP)]
            near_in = [sem(f"near_in{u}") for u in range(GROUP)]
            ones_set = sem("ones_set")
            v_ones_set = sem("v_ones_set")
            score_ready = sem("score_ready")
            drained = sem("drained")
            near_done = sem("near_done")
            pv_done = sem("pv_done")
            v_read = sem("v_read")
            v_built = sem("v_built")
            neg_done = sem("neg_done")
            shift_turned = sem("shift_turned")
            o_copied = sem("o_copied")
            o_turned = sem("o_turned")
            recip_done = sem("recip_done")
            o_done = sem("o_done")

            def near_span(kb):
                first = P * kb - NEAR
                return max(first, 0), min(first + NQ, S), max(-first, 0)

            RING = 3
            MAX_BANK = RING
            SUM_BANK = 7
            TURN_RESULT, TURN_SHIFT = 3, 13
            RESULT_AT = CPB * TURN_RESULT
            SHIFT_AT = CPB * TURN_SHIFT + 1
            RING_TILES = CPB * KB + 2

            def tile_at(kb, c):
                return CPB * kb + c + (kb >= TURN_RESULT) + (kb >= TURN_SHIFT)

            def drained_at(n, at):
                count = RING_TILES * n + at + 1
                if isinstance(n, int):
                    count += (n == 0 and at < RESULT_AT) - (n == NH - 1 and at >= SHIFT_AT)
                return count

            def max_at(n, step):
                return (n + 1, step + LEAD) if step + LEAD < KB else (n + 2, step + LEAD - KB)

            block = c2.enter_context(nc.Block())

            @block.sync
            def _(sp):
                def load(n, u):
                    wait(sp, score_ready, CPB * KB * (n - GROUP + 1))
                    load_stacks(sp, n, q_st[u], k_st[u], stacks_in[u])
                    wait(sp, near_done, KB * (n - GROUP + 1))
                    sp.dma_start(near[u][:], near_d[bass.ds(n % H, 1)].rearrange("a p c -> (a p) c")).then_inc(near_in[u], 16)

                def shift(n, u):
                    wait(sp, drained, 1 if isinstance(n, int) and n == 0 else drained_at(n - 1, SHIFT_AT))
                    sp.dma_start(q_st[u][ROWS:ROWS + 1, :].rearrange("a (i p) -> a i p", p=P), shift_row[:, n % 2 if isinstance(n, int) else u % 2, :]) \
                        .then_inc(shift_in[u], 16)

                def group(g, last=False):
                    for u in range(GROUP):
                        n = GROUP * g + u
                        if not (last and u > 0):
                            load(n + GROUP - 1, (u + GROUP - 1) % GROUP)
                        if not (last and u == GROUP - 1):
                            shift(n + 1, (u + 1) % GROUP)

                load(0, 0)
                shift(0, 0)
                for u in range(1, GROUP - 1):
                    load(u, u)
                group(0)
                with sp.Fori(1, GROUPS - 1) as g:
                    group(g)
                group(GROUPS - 1, last=True)

            @block.scalar
            def _(act):
                def shift(n, par):
                    wait(act, shift_turned, n + 1)
                    nc.scalar.activation(shift_row[:, par % 2, :], ps[0:KB, SHIFT_AT % RING, 0:P], ACT.Copy).then_inc(drained, 1)

                def collect(n):
                    wait(act, pv_done, CPB * KB * (n + 1))
                    wait(act, o_turned, n)
                    nc.scalar.activation(o_sb[:], ps[:, SUM_BANK], ACT.Copy).then_inc(o_copied, 1)

                def collect_turned(n):
                    wait(act, o_turned, n + 1)
                    wait(act, o_done, n)
                    nc.scalar.activation(o_turned_sb[:].rearrange("p i c w -> p (i c w)"), ps[:, RESULT_AT % RING], ACT.Copy) \
                        .then_inc(drained, 1)

                def head(n, u, first=False, last=False):
                    for kb in range(KB):
                        if kb == 1 and not first:
                            collect(n - 1)
                        if kb == TURN_RESULT and not first:
                            collect_turned(n - 1)
                        if kb == TURN_SHIFT and not last:
                            shift(n + 1, (u + 1) % GROUP)
                        for c in range(CPB):
                            i = CPB * (KB * n + kb) + c
                            wait(act, score_ready, i + 1)
                            wait(act, pv_done, i - 2 * CPB + 1)
                            nc.scalar.activation(prob[:, kb % 2, CH * c:CH * (c + 1)], ps[:, tile_at(kb, c) % RING], ACT.Exp).then_inc(drained, 1)

                shift(0, 0)
                for u in range(GROUP):
                    head(u, u, first=u == 0)
                with act.Fori(1, GROUPS - 1) as g:
                    for u in range(GROUP):
                        head(GROUP * g + u, u)
                for u in range(GROUP):
                    head(NH - GROUP + u, u, last=u == GROUP - 1)
                collect(NH - 1)
                collect_turned(NH - 1)

            @block.gpsimd
            def _(pool):
                def build(n, u, turn):
                    wait(pool, pv_done, CPB * KB * (n - 1))
                    pool.wait_ge(v_ones_set, 2)
                    nc.gpsimd.tensor_copy(vx[:, u % 2, :, 0:D], v_all[:, bass.ds(n, 1)].rearrange("p a k d -> p (a k) d")) \
                        .then_inc(v_read, 1)
                    pool.wait_ge(near_in[u], 16 * turn)
                    wait(pool, v_read, n + 1)
                    nc.gpsimd.tensor_tensor(vr[:, u % 2], vx[:, u % 2],
                                            near[u][:, 0:1].unsqueeze(2).to_broadcast([P, KB, 32]), ALU.mult).then_inc(v_built, 1)

                def normalise(n):
                    nc.gpsimd.tensor_tensor(
                        v_all[:, bass.ds(n, 1)].rearrange("p a (c i) d -> p i (a c) d", c=CPB), o_turned_sb[:, :, :, 0:D],
                        recip[:].unsqueeze(3).to_broadcast([P, TPC, CPB, D]), ALU.mult).then_inc(o_done, 1)

                def head(g, u, first=False, last=False):
                    n = GROUP * g + u
                    for kb in range(KB):
                        if kb == TURN_RESULT + 2 and not first:
                            wait(pool, recip_done, n)
                            wait(pool, v_read, n)
                        if kb == 8 and not last:
                            build(n + 1, (u + 1) % GROUP, g + 1 if u + 1 < GROUP else g + 2)
                        q0, q1, c0 = near_span(kb)
                        wait(pool, drained, drained_at(n, tile_at(kb, (q1 - 1) // CH)))
                        nc.gpsimd.tensor_tensor(prob[:, kb % 2, q0:q1], prob[:, kb % 2, q0:q1], near[u][:, c0:c0 + q1 - q0],
                                                ALU.mult).then_inc(near_done, 1)
                        if kb == TURN_RESULT + 2 and not first:
                            normalise(n - 1)

                nc.gpsimd.memset(vx[:, :, :, D + 1:32], 0.0).then_inc(v_ones_set, 1)
                nc.gpsimd.memset(vx[:, :, :, D:D + 1], 1.0).then_inc(v_ones_set, 1)
                build(0, 0, 1)
                for u in range(GROUP):
                    head(0, u, first=u == 0)
                with pool.Fori(1, GROUPS - 1) as g:
                    for u in range(GROUP):
                        head(g, u)
                for u in range(GROUP):
                    head(GROUPS - 1, u, last=u == GROUP - 1)
                wait(pool, recip_done, NH)
                wait(pool, v_read, NH)
                normalise(NH - 1)

            @block.vector
            def _(dve):
                def maxima(m, par, i):
                    for half in range(2):
                        wait(dve, max_ready, 2 * (KB * m + i) + half + 1)
                        if i == 0 and half == 0:
                            wait(dve, neg_done, m - 1)
                        nc.vector.reduce_max(max_half[:, par % 2, i, half:half + 1],
                                             ps[:, MAX_BANK + 2 * half:MAX_BANK + 2 + 2 * half].rearrange("p a n -> p (a n)"), AX.X).then_inc(max_done, 1)

                def combine(m, par):
                    wait(dve, max_done, 2 * KB * (m + 1))
                    wait(dve, shift_turned, m - 1)
                    nc.vector.tensor_reduce(max_neg[:, par % 2], max_half[:, par % 2], AX.X, ALU.max, negate=True).then_inc(neg_done, 1)

                def reciprocals(n, copied):
                    wait(dve, drained, copied)
                    wait(dve, o_done, n)
                    nc.vector.reciprocal(recip[:], o_turned_sb[:, :, :, D]).then_inc(recip_done, 1)

                def head(n, u, first=False, left=2):
                    for kb in range(KB):
                        ahead = 1 if kb + LEAD < KB else 2
                        m, i = max_at(n, kb)
                        if ahead <= left:
                            maxima(m, (u + ahead) % 2, i)
                        if kb == TURN_RESULT and not first:
                            reciprocals(n - 1, drained_at(n, RESULT_AT))
                        if kb == KB - 1 - LEAD and left >= 1:
                            combine(n + 1, u + 1)

                combine(0, 0)
                for u in range(GROUP):
                    nc.vector.memset(k_st[u][ROWS:ROWS + 1, :], 1.0).then_inc(ones_set, 1)
                for u in range(GROUP):
                    head(u, u, first=u == 0)
                with dve.Fori(1, GROUPS - 1) as g:
                    for u in range(GROUP):
                        head(GROUP * g + u, u)
                for u in range(GROUP):
                    head(NH - GROUP + u, u, left=GROUP - 1 - u)
                reciprocals(NH - 1, drained_at(NH - 1, RING_TILES - 1) + 1)

            @block.tensor
            def _(pe):
                def maxima(m, u, i, c):
                    if c % 2 == 0:
                        wait(pe, max_done, 2 * (KB * m + i) + c // 2 - 1)
                    mm = nc.tensor.matmul(ps[:, MAX_BANK + c], q_st[u][0:ROWS, P * i:P * (i + 1)], k_st[u][0:ROWS, CH * c:CH * (c + 1)],
                                          start=True, stop=True)
                    if c % 2 == 1:
                        mm.then_inc(max_ready, 1)

                def ring_free(n, at):
                    wait(pe, drained, drained_at(n, at - RING))

                def turn_shift(m, par):
                    wait(pe, neg_done, m + 1)
                    nc.tensor.transpose(ps[0:KB, SHIFT_AT % RING, 0:P], max_neg[:, par % 2], ident[:]).then_inc(shift_turned, 1)

                def scores(n, u, kb, c):
                    ring_free(n, tile_at(kb, c))
                    nc.tensor.matmul(ps[:, tile_at(kb, c) % RING], k_st[u][:, P * kb:P * (kb + 1)], q_st[u][:, CH * c:CH * (c + 1)],
                                     start=True, stop=True).then_inc(score_ready, 1)

                def values(n, u, kb, c):
                    q0, q1, _ = near_span(kb)
                    lo, hi = CH * c, CH * (c + 1)
                    if q0 < hi and q1 > lo:
                        wait(pe, near_done, KB * n + kb + 1)
                    else:
                        wait(pe, drained, drained_at(n, tile_at(kb, c)))
                    if kb == 0 and c == 0:
                        wait(pe, v_built, n + 1)
                        wait(pe, o_copied, n)
                    cut = min(max(P * kb - NEAR, lo), hi)
                    for v, a, z in ((vr, lo, cut), (vx, cut, hi)):
                        if a < z:
                            last = nc.tensor.matmul(ps[32 * c:32 * (c + 1), SUM_BANK, a - lo:z - lo], v[:, u % 2, kb],
                                                    prob[:, kb % 2, a:z], start=kb == 0, stop=kb == KB - 1 and z == hi)
                    last.then_inc(pv_done, 1)

                def turn_result(n):
                    wait(pe, o_copied, n + 1)
                    for i in range(TPC):
                        last = nc.tensor.transpose(ps[:, RESULT_AT % RING, P * i:P * (i + 1)], o_sb[:, P * i:P * (i + 1)], ident[:])
                    last.then_inc(o_turned, 1)

                def sums(n, u, kb, first):
                    for c in range(CPB):
                        if kb > 0:
                            values(n, u, kb - 1, c)
                        elif not first:
                            values(n - 1, u + 1, KB - 1, c)

                def head(g, u, first=False, left=2):
                    n = GROUP * g + u
                    for kb in range(KB):
                        ahead = 1 if kb + LEAD < KB else 2
                        m, i = max_at(n, kb)
                        mu = (u + ahead) % GROUP
                        if kb == 0:
                            pe.wait_ge(shift_in[u], 16 * (g + 1))
                            if isinstance(g, int) and g == 0:
                                pe.wait_ge(ones_set, u + 1)
                        if i == 0 and ahead <= left:
                            pe.wait_ge(stacks_in[mu], 16 * STACK_LOADS * (g + 1 + (u + ahead) // GROUP))
                        if kb == TURN_RESULT and not first:
                            ring_free(n, RESULT_AT)
                            turn_result(n - 1)
                        if kb == TURN_SHIFT and left >= 1:
                            ring_free(n, SHIFT_AT)
                            turn_shift(n + 1, u + 1)
                        for c in range(CPB):
                            scores(n, u, kb, c)
                            if c == CPB // 2:
                                sums(n, u, kb, first)
                            if first and kb == 0 and c == 0:
                                pe.wait_ge(stacks_in[1], 16 * STACK_LOADS)
                            if ahead <= left:
                                maxima(m, mu, i, c)

                turn_shift(0, 0)
                pe.wait_ge(stacks_in[0], 16 * STACK_LOADS)
                for u in range(GROUP):
                    head(0, u, first=u == 0)
                with pe.Fori(1, GROUPS - 1) as g:
                    for u in range(GROUP):
                        head(g, u)
                for u in range(GROUP):
                    head(GROUPS - 1, u, left=GROUP - 1 - u)
                for c in range(CPB):
                    values(NH - 1, NH - 1, KB - 1, c)
                ring_free(NH - 1, RING_TILES - 1 + RING)
                turn_result(NH - 1)

        c3 = ExitStack()
        with c3:
            wo_raw = sb("wo_raw", [P, KE, E], c=c3)
            wo_parts = sb("wo_parts", [P, 2, KE, E], F32R, c=c3)
            base_in = sb("base_in", [P, CPB, TPC, E], c=c3)
            rows = sb("rows", [P, 2, TPC, E], c=c3)
            turned = sb("turned", [P, 2, 2, KE, CH], F32R, c=c3)

            wo_in = sem("wo_in")
            wo_high = sem("wo_high")
            wo_low = sem("wo_low")
            rows_in = [sem(f"rows_in{i}") for i in range(CPB)]
            packed = sem("packed")
            a_turned = sem("a_turned")
            a_high = sem("a_high")
            a_low = sem("a_low")
            proj_ready = sem("proj_ready")
            res_done = sem("res_done")
            stored = [sem(f"stored{i}") for i in range(CPB)]
            TURN_BANKS = [0, 6]
            PROJ_BANK = 2

            def ahead(b, c, by):
                nb, nc_ = b + (c + by) // CPB, (c + by) % CPB
                return nb, nc_, not isinstance(b, int) or nb < B

            block = c3.enter_context(nc.Block())

            @block.sync
            def _(sp):
                def load(b, c):
                    wait(sp, stored[c], 16 * b)
                    sp.dma_start(base_in[:, c], base_d[bass.ds(S * b + CH * c, CH), :].rearrange("(t p) e -> p t e", p=P)) \
                        .then_inc(rows_in[c], 16)

                def batch(b):
                    for c in range(CPB):
                        wait(sp, res_done, TPC * (CPB * b + c + 1))
                        sp.dma_start(out[bass.ds(S * b + CH * c, CH), :].rearrange("(t p) e -> p t e", p=P), base_in[:, c]) \
                            .then_inc(stored[c], 16)
                        nb, nc_, there = ahead(b, c, CPB - 1)
                        if there:
                            load(nb, nc_)

                sp.dma_start(wo_raw[:], w_out.rearrange("(k p) n -> p k n", p=P)).then_inc(wo_in, 16)
                for c in range(CPB - 1):
                    load(0, c)
                batch(0)
                with sp.Fori(1, B - 1) as b:
                    batch(b)
                batch(B - 1)
                for c in range(CPB):
                    sp.wait_ge(stored[c], 16 * B)

            @block.scalar
            def _(act):
                def pack(b, c):
                    n = CPB * b + c
                    wait(act, a_turned, n - 1)
                    for t in range(TPC):
                        last = nc.scalar.activation(rows[:, c % 2, t].rearrange("p (h d) -> p h d", d=D),
                                                    v_all[:, bass.ds(H * b, H), TPC * c + t, :], ACT.Copy)
                    last.then_inc(packed, 1)

                def batch(b):
                    for c in range(CPB):
                        n = CPB * b + c
                        for k in range(KE):
                            wait(act, a_turned, n + 1)
                            wait(act, proj_ready, TPC * (n - 1))
                            nc.scalar.activation(turned[:, c % 2, 0, k], ps[:, TURN_BANKS[c % 2] + k], ACT.Copy).then_inc(a_high, 1)
                        nb, nc_, there = ahead(b, c, 2)
                        if there:
                            pack(nb, nc_)

                pack(0, 0)
                act.wait_ge(wo_in, 16)
                nc.scalar.activation(wo_parts[:, 0], wo_raw[:], ACT.Copy).then_inc(wo_high, 1)
                pack(0, 1)
                batch(0)
                with act.Fori(1, B - 1) as b:
                    batch(b)
                batch(B - 1)

            @block.vector
            def _(dve):
                def low(n, c):
                    for k in range(KE):
                        wait(dve, a_high, KE * n + k + 1)
                        nc.vector.tensor_tensor(turned[:, c % 2, 1, k], ps[:, TURN_BANKS[c % 2] + k], turned[:, c % 2, 0, k].bitcast(F32),
                                                ALU.subtract).then_inc(a_low, 1)

                def batch(b):
                    for c in range(CPB):
                        n = CPB * b + c
                        if ahead(b, c, 1)[2]:
                            low(n + 1, c + 1)
                        for t in range(TPC):
                            wait(dve, proj_ready, TPC * n + t + 1)
                            if t == 0:
                                wait(dve, rows_in[c], 16 * (b + 1))
                            nc.vector.tensor_tensor(base_in[:, c, t], base_in[:, c, t], ps[:, PROJ_BANK + t, 0:E], ALU.add) \
                                .then_inc(res_done, 1)

                dve.wait_ge(wo_high, 1)
                nc.vector.tensor_tensor(wo_parts[:, 1], wo_raw[:], wo_parts[:, 0].bitcast(F32), ALU.subtract).then_inc(wo_low, 1)
                low(0, 0)
                batch(0)
                with dve.Fori(1, B - 1) as b:
                    batch(b)
                batch(B - 1)

            @block.tensor
            def _(pe):
                def turn(n, c):
                    wait(pe, packed, n + 1)
                    wait(pe, a_low, KE * (n - 1))
                    for t in range(TPC):
                        for k in range(KE):
                            last = nc.tensor.transpose(ps[:, TURN_BANKS[c % 2] + k, P * t:P * (t + 1)], rows[:, c % 2, t, P * k:P * (k + 1)],
                                                       ident[:])
                    last.then_inc(a_turned, 1)

                def batch(b):
                    for c in range(CPB):
                        n = CPB * b + c
                        wait(pe, a_low, KE * (n + 1))
                        for t in range(TPC):
                            wait(pe, res_done, TPC * (n - 1) + t + 1)
                            for k in range(KE):
                                for i, j in PASSES:
                                    last = nc.tensor.matmul(ps[:, PROJ_BANK + t, 0:E], turned[:, c % 2, i, k, P * t:P * (t + 1)],
                                                            wo_parts[:, j, k], start=k == 0 and (i, j) == PASSES[0],
                                                            stop=k == KE - 1 and (i, j) == PASSES[-1])
                            last.then_inc(proj_ready, 1)
                        if ahead(b, c, 2)[2]:
                            turn(n + 2, c)

                turn(0, 0)
                turn(1, 1)
                pe.wait_ge(wo_low, 1)
                batch(0)
                with pe.Fori(1, B - 1) as b:
                    batch(b)
                batch(B - 1)


_INS = ["L0_attn_hidden_states", "L0_attn_W_qkv", "L0_attn_W_out", "L0_attn_rel_emb", "L0_ffn_router_w",
        "L0_ffn_w1", "L0_ffn_b1", "L0_ffn_w2", "L0_ffn_b2"]


def kernel(**inputs):
    import numpy as np
    import concourse.bacc as bacc
    from concourse.bass_utils import run_bass_kernel_spmd

    nc = bacc.Bacc("TRN2", target_bir_lowering=False, num_devices=1)
    arrays, args = {}, []
    for name in _INS + ["bucket_line"]:
        a = bucket_line() if name == "bucket_line" else np.ascontiguousarray(inputs[name])
        if name == _INS[0]:
            a = a.reshape(B * S, E)
        arrays[f"in_{name}"] = a
        args.append(nc.dram_tensor(f"in_{name}", a.shape, mybir.dt.from_np(a.dtype), kind="ExternalInput").ap())
    args.append(nc.dram_tensor("out_rows", (B * S, E), F32, kind="ExternalOutput").ap())
    transformer_layer(nc, *args)
    r = run_bass_kernel_spmd(nc, [arrays], core_ids=[0])
    return r.results[0]["out_rows"].reshape(B, S, E)
```
